# Optimizing a Trainium2 kernel written in Bass

```python
import numpy as np
import jax
import jax.numpy as jnp

def _softmax(x, axis=-1):
    return jax.nn.softmax(x, axis=axis)

def _gelu(x):
    return jax.nn.gelu(x, approximate=True)

def _silu(x):
    return jax.nn.silu(x)

def _sigmoid(x):
    return jax.nn.sigmoid(x)

def _layernorm(x, axis=-1, eps=1e-05):
    m = jnp.mean(x, axis=axis, keepdims=True)
    v = jnp.var(x, axis=axis, keepdims=True)
    return (x - m) / jnp.sqrt(v + eps)

def _scatter_add(tgt, idx, src, axis=0):
    return tgt.at[idx].add(src)

def _segment_sum(src, seg, n):
    return jax.ops.segment_sum(src, seg, n)
kernel_name = 'mk_adj_ffn_d1_adj_r2_6547b9'

def setup_inputs(seed: int=0):
    np.random.seed(seed)
    _w = jnp.asarray

    def _rec_inputs():
        import jax
        import jax.numpy as jnp
        _gk = jax.random.key(seed)
        x = -0.0002928 + 1 * jax.random.normal(jax.random.fold_in(_gk, 1), (8192, 256), jnp.float32)
        _a = jax.random.bernoulli(jax.random.fold_in(_gk, 2), 0.000244141, (8192, 8192))
        adj = _a.astype(jnp.int32)
        return (x, adj)
    x, adj = _rec_inputs()

    def _L0_gnn_setup():
        import jax, jax.numpy as jnp
        import numpy as np
        key = jax.random.key(seed)
        kX, kA, k1, k2, k3, k4 = jax.random.split(key, 6)
        N, Cin, Cout = (4096, 256, 256)
        X = jax.random.normal(kX, (N, Cin), dtype=jnp.float32)
        A = jax.random.randint(kA, (N, N), 0, 2, dtype=jnp.int32)
        bound = 1.0 / np.sqrt(Cin)
        W_nb = jax.random.uniform(k1, (Cout, Cin), jnp.float32, -bound, bound)
        b_nb = jax.random.uniform(k2, (Cout,), jnp.float32, -bound, bound)
        W_line = jax.random.uniform(k3, (Cout, Cin), jnp.float32, -bound, bound)
        b_line = jax.random.uniform(k4, (Cout,), jnp.float32, -bound, bound)
        return {'X': X, 'A': A, 'W_nb': W_nb, 'b_nb': b_nb, 'W_line': W_line, 'b_line': b_line, 'neibor_num': 64}
    _L0_gnn_all = _L0_gnn_setup()
    _L0_gnn_in = {k: v for k, v in _L0_gnn_all.items() if k in ('W_nb', 'b_nb', 'W_line', 'b_line')}
    del _L0_gnn_all

    def _L0_ffn_setup():
        import jax, jax.numpy as jnp
        import numpy as np
        E = 64
        K = 8
        D = 256
        I = 512
        C = 512

        def _moe_forward(x, gate_w, adaptive_bias, w1, w3, w2, ws1, ws3, ws2):
            B, S, _ = x.shape
            T = B * S
            xf = x.reshape(T, D)
            scores = xf @ gate_w.T + adaptive_bias
            probs = jax.nn.softmax(scores, axis=-1)
            topw, topi = jax.lax.top_k(probs, K)
            topw = topw / (jnp.sum(topw, axis=-1, keepdims=True) + 1e-08)
            flat_e = topi.reshape(-1)
            flat_w = topw.reshape(-1)
            flat_t = jnp.repeat(jnp.arange(T), K)
            order = jnp.argsort(flat_e)
            counts = jnp.bincount(flat_e, length=E)
            offsets = jnp.cumsum(counts) - counts
            slot_sorted = jnp.arange(T * K) - offsets[flat_e[order]]
            slot = jnp.zeros(T * K, jnp.int32).at[order].set(slot_sorted.astype(jnp.int32))
            valid = slot < C
            slot_c = jnp.clip(slot, 0, C - 1)
            xg = xf[flat_t] * valid[:, None].astype(xf.dtype)
            buf = jnp.zeros((E, C, D), xf.dtype).at[flat_e, slot_c].add(xg)
            h = jax.nn.silu(jnp.einsum('ecd,edi->eci', buf, w1)) * jnp.einsum('ecd,edi->eci', buf, w3)
            y = jnp.einsum('eci,eid->ecd', h, w2)
            pair_out = y[flat_e, slot_c] * (flat_w * valid.astype(flat_w.dtype))[:, None]
            out = jnp.zeros_like(xf).at[flat_t].add(pair_out)
            shared = jax.nn.silu(xf @ ws1) * (xf @ ws3) @ ws2
            return (out + shared).reshape(B, S, D)
        key = jax.random.key(seed)
        ks = jax.random.split(key, 9)
        B, S = (2, 512)
        s_in = 1.0 / np.sqrt(D)
        s_mid = 1.0 / np.sqrt(I)
        return {'x': jax.random.normal(ks[0], (B, S, D), jnp.float32), 'gate_w': jax.random.normal(ks[1], (E, D), jnp.float32) * 0.02, 'adaptive_bias': jnp.zeros((E,), jnp.float32), 'w1': jax.random.normal(ks[2], (E, D, I), jnp.float32) * s_in, 'w3': jax.random.normal(ks[3], (E, D, I), jnp.float32) * s_in, 'w2': jax.random.normal(ks[4], (E, I, D), jnp.float32) * s_mid, 'ws1': jax.random.normal(ks[5], (D, I), jnp.float32) * s_in, 'ws3': jax.random.normal(ks[6], (D, I), jnp.float32) * s_in, 'ws2': jax.random.normal(ks[7], (I, D), jnp.float32) * s_mid}
    _L0_ffn_all = _L0_ffn_setup()
    _L0_ffn_in = {k: v for k, v in _L0_ffn_all.items() if k in ('gate_w', 'adaptive_bias', 'w1', 'w3', 'w2', 'ws1', 'ws3', 'ws2')}
    del _L0_ffn_all
    return {'x': x, 'adj': adj, 'L0_gnn_W_nb': _L0_gnn_in['W_nb'], 'L0_gnn_b_nb': _L0_gnn_in['b_nb'], 'L0_gnn_W_line': _L0_gnn_in['W_line'], 'L0_gnn_b_line': _L0_gnn_in['b_line'], 'L0_ffn_gate_w': _L0_ffn_in['gate_w'], 'L0_ffn_adaptive_bias': _L0_ffn_in['adaptive_bias'], 'L0_ffn_w1': _L0_ffn_in['w1'], 'L0_ffn_w3': _L0_ffn_in['w3'], 'L0_ffn_w2': _L0_ffn_in['w2'], 'L0_ffn_ws1': _L0_ffn_in['ws1'], 'L0_ffn_ws3': _L0_ffn_in['ws3'], 'L0_ffn_ws2': _L0_ffn_in['ws2']}

def reference(x, adj, L0_gnn_W_nb, L0_gnn_b_nb, L0_gnn_W_line, L0_gnn_b_line, L0_ffn_gate_w, L0_ffn_adaptive_bias, L0_ffn_w1, L0_ffn_w3, L0_ffn_w2, L0_ffn_ws1, L0_ffn_ws3, L0_ffn_ws2):
    import jax
    import jax.numpy as jnp

    def _L0_gnn_ref(X, A, W_nb, b_nb, W_line, b_line, neibor_num):
        import jax, jax.numpy as jnp
        import numpy as np
        Ab = A > 0
        keep = Ab & (jnp.cumsum(Ab.astype(jnp.int32), axis=1) <= neibor_num)
        cnt = keep.sum(axis=1, keepdims=True).astype(X.dtype)
        nb_sum = keep.astype(X.dtype) @ X
        nb_mean = nb_sum / jnp.maximum(cnt, 1.0)
        xj = jax.nn.leaky_relu(nb_mean @ W_nb.T + b_nb)
        xi = jax.nn.leaky_relu(X @ W_line.T + b_line)
        return xi + jnp.where(cnt > 0, xj, jnp.zeros((), X.dtype))

    def _L0_ffn_ref(x, gate_w, adaptive_bias, w1, w3, w2, ws1, ws3, ws2):
        import jax, jax.numpy as jnp
        import numpy as np
        E = 64
        K = 8
        D = 256
        I = 512
        C = 512

        def _moe_forward(x, gate_w, adaptive_bias, w1, w3, w2, ws1, ws3, ws2):
            B, S, _ = x.shape
            T = B * S
            xf = x.reshape(T, D)
            scores = xf @ gate_w.T + adaptive_bias
            probs = jax.nn.softmax(scores, axis=-1)
            topw, topi = jax.lax.top_k(probs, K)
            topw = topw / (jnp.sum(topw, axis=-1, keepdims=True) + 1e-08)
            flat_e = topi.reshape(-1)
            flat_w = topw.reshape(-1)
            flat_t = jnp.repeat(jnp.arange(T), K)
            order = jnp.argsort(flat_e)
            counts = jnp.bincount(flat_e, length=E)
            offsets = jnp.cumsum(counts) - counts
            slot_sorted = jnp.arange(T * K) - offsets[flat_e[order]]
            slot = jnp.zeros(T * K, jnp.int32).at[order].set(slot_sorted.astype(jnp.int32))
            valid = slot < C
            slot_c = jnp.clip(slot, 0, C - 1)
            xg = xf[flat_t] * valid[:, None].astype(xf.dtype)
            buf = jnp.zeros((E, C, D), xf.dtype).at[flat_e, slot_c].add(xg)
            h = jax.nn.silu(jnp.einsum('ecd,edi->eci', buf, w1)) * jnp.einsum('ecd,edi->eci', buf, w3)
            y = jnp.einsum('eci,eid->ecd', h, w2)
            pair_out = y[flat_e, slot_c] * (flat_w * valid.astype(flat_w.dtype))[:, None]
            out = jnp.zeros_like(xf).at[flat_t].add(pair_out)
            shared = jax.nn.silu(xf @ ws1) * (xf @ ws3) @ ws2
            return (out + shared).reshape(B, S, D)
        return _moe_forward(x, gate_w, adaptive_bias, w1, w3, w2, ws1, ws3, ws2)
    x = x + _L0_gnn_ref(_layernorm(x, axis=-1), adj, L0_gnn_W_nb, L0_gnn_b_nb, L0_gnn_W_line, L0_gnn_b_line, 64)
    x = x + _L0_ffn_ref(_layernorm(x, axis=-1)[None], L0_ffn_gate_w, L0_ffn_adaptive_bias, L0_ffn_w1, L0_ffn_w3, L0_ffn_w2, L0_ffn_ws1, L0_ffn_ws3, L0_ffn_ws2)[0]
    return x

_drawn_inputs = setup_inputs


def setup_inputs(seed=0):
    import zlib

    import numpy as np

    out = dict(_drawn_inputs(seed))
    spreads = {'L0_ffn_adaptive_bias': (0.0, 0.1)}
    factors = {}
    for name, (base, spread) in spreads.items():
        noise = np.random.default_rng([zlib.crc32(name.encode()), seed]).standard_normal(out[name].shape)
        drawn = base * np.exp(spread * noise) if base else spread * noise
        out[name] = jnp.asarray(drawn.astype(out[name].dtype))
    for name, factor in factors.items():
        out[name] = (out[name] * factor).astype(out[name].dtype)
    return out
```

```python
import concourse.bass as bass
from concourse import mybir
from contextlib import ExitStack


class Tile:

    UNROLL = 4

    def __init__(self, g, j):
        self.g, self.j = g + j // self.UNROLL, j % self.UNROLL
        self.n = self.UNROLL * self.g + self.j

    def back(self, lag):
        return Tile(self.g, self.j - lag)

    def slot(self, ring):
        return self.j % ring

    def round(self, ring):
        return (self.UNROLL // ring) * self.g + self.j // ring

    def at_least(self, k):
        return self.n >= k if isinstance(self.n, int) else True


def run_steps(eng, steps, tiles, max_lag, step):
    u = Tile.UNROLL
    assert tiles % u == 0 and max_lag <= u and steps == tiles + max_lag
    for j in range(2 * u):
        step(Tile(0, j), lambda lag, j=j: 0 <= j - lag)
    with eng.Fori(2, tiles // u - 1) as g:
        for j in range(u):
            step(Tile(g, j), lambda lag: True)
    for j in range(u + max_lag):
        step(Tile(tiles // u - 1, j), lambda lag, j=j: j - lag < u)


def apart(eng):
    eng.nop(nofuse=True)


class Chain:

    def __init__(self, eng, sem, base):
        self.eng, self.sem, self.base, self.n = eng, sem, base, 0

    def did(self, instruction):
        instruction.then_inc(self.sem, 1)
        self.n += 1

    def wait(self):
        self.eng.wait_ge(self.sem, self.base + self.n)


def graph_moe_kernel(nc, x, adj, w_nb_t, b_nb, w_line_t, b_line, gate_t, gate_b,
                     w1, w3, w2, ws1, ws3, ws2, out):
    fp32, bf16, i32, u32 = mybir.dt.float32, mybir.dt.bfloat16, mybir.dt.int32, mybir.dt.uint32
    ALU = mybir.AluOpType
    ACT = mybir.ActivationFunctionType
    AX_X = mybir.AxisListType.X

    P = 128
    T, D = x.shape
    E, _, I = w1.shape
    C = out.shape[0] - T
    NT = T // P
    DC = D // P
    IC = I // P
    CQ = C // P
    TOPK = 8
    NBR = 8
    CAP = 64
    ROUNDS = CAP // NBR - 1
    ROW = D + E
    EPS = 1e-5
    NEWTON = 3
    BIG = 131072
    assert BIG > E * C and DC == 2 and IC == 4 and CQ == 4

    xn_d = nc.dram_tensor("xn_d", (T, D), fp32, kind="Internal").ap()
    rows_d = nc.dram_tensor("rows_d", (T + C, ROW), fp32, kind="Internal").ap()
    table_d = nc.dram_tensor("table_d", (E * C, 1), i32, kind="Internal").ap()

    ctx = ExitStack()
    with ctx:
        def sb(name, shape, dt=fp32):
            return ctx.enter_context(nc.sbuf_tensor(name, shape, dt))

        def sem(name):
            return ctx.enter_context(nc.semaphore(name))

        ident = sb("ident", [P, P])
        before = sb("before", [P, P], bf16)
        ones_bf = sb("ones_bf", [P, P], bf16)
        ones8 = sb("ones8", [P, NBR], bf16)
        ones_row = sb("ones_row", [1, P])
        zeros = sb("zeros", [P, CQ * ROW])
        slot_code = sb("slot_code", [P, E])
        token_ids = sb("token_ids", [P, NT], i32)
        spare_ids = sb("spare_ids", [E, C], i32)
        w_line_sb = sb("w_line_sb", [P, DC, D])
        w_nb_sb = sb("w_nb_sb", [P, DC, D])
        gate_sb = sb("gate_sb", [P, DC, E])
        gate_b_sb = sb("gate_b_sb", [1, E])
        bias_sb = sb("bias_sb", [1, 2 * D])
        ws1_sb = sb("ws1_sb", [P, DC, I])
        ws3_sb = sb("ws3_sb", [P, DC, I])
        ws2_sb = sb("ws2_sb", [P, IC, D])

        adj_sb = sb("adj_sb", [P, 2, T], i32)
        sign_sb = sb("sign_sb", [P, 2, T + NBR], bf16)
        near = sb("near", [P, 2, NBR, D])
        more = sb("more", [P, NBR, D])
        idx = [sb(f"idx{s}", [P, NBR], u32) for s in range(2)]
        idx_more = sb("idx_more", [P, NBR], u32)
        minus_half = sb("minus_half", [P, 1])
        sign_sum = sb("sign_sum", [P, 2])
        too_many = sb("too_many", [P, ROUNDS])
        full = sb("full", [P, ROUNDS], bf16)
        flags = sb("flags", [1, ROUNDS], i32)
        count = sb("count", [P, 1])
        x_sb = sb("x_sb", [P, 4, D])
        xn_sb = sb("xn_sb", [P, 4, D])
        sums_t = sb("sums_t", [P, 2 * DC, P])
        cnt1 = sb("cnt1", [P, 1])
        inv_cnt = sb("inv_cnt", [P, 1])
        any_nb = sb("any_nb", [P, 4, 1])
        mean_diag = sb("mean_diag", [P, P])
        z_sb = sb("z_sb", [P, 2 * D])
        lz_sb = sb("lz_sb", [P, 2 * D])
        x1 = sb("x1", [P, 4, D])
        stats = sb("stats", [P, 6])
        mv = sb("mv", [P, 2])
        rstd = sb("rstd", [P, 1])
        root_sb = sb("root_sb", [P, 2])
        row = [sb(f"row{s}", [P, ROW]) for s in range(4)]
        xf_t = sb("xf_t", [P, DC, P])
        mx8 = sb("mx8", [P, 8])
        neg_max = sb("neg_max", [P, 1])
        e_sb = sb("e_sb", [P, E])
        e_sum = sb("e_sum", [P, 1])
        inv_sum = sb("inv_sum", [P, 1])
        probs = sb("probs", [P, E])
        top8 = sb("top8", [P, 8])
        struck = sb("struck", [P, E])
        mask = sb("mask", [P, 2, E], bf16)
        mask_sum = sb("mask_sum", [P, E], bf16)
        top_sum = sb("top_sum", [P, 1])
        top_sum_eps = sb("top_sum_eps", [P, 1])
        inv_top = sb("inv_top", [P, 1])
        sel = sb("sel", [P, E])
        code = sb("code", [P, E])
        code_sel = sb("code_sel", [P, E])
        code8 = sb("code8", [P, TOPK])
        dest = [sb(f"dest{s}", [P, TOPK], u32) for s in range(4)]
        token = [sb(f"token{s}", [P, 1], i32) for s in range(4)]
        tanh_sb = sb("tanh_sb", [P, I])
        u_sb = sb("u_sb", [P, I])
        g_sb = sb("g_sb", [P, I])
        h_t = sb("h_t", [P, IC, P])
        base = sb("base", [P, 2, D])

        pool32 = adj_sb[:, :, :].rearrange("p s n -> p (s n)").bitcast(fp32)
        at = [0]

        def over(n):
            at[0] += n
            assert at[0] <= 2 * T
            return pool32[:, at[0] - n:at[0]]

        w1_sb = [over(DC * I).rearrange("p (k i) -> p k i", k=DC) for _ in range(2)]
        w3_sb = [over(DC * I).rearrange("p (k i) -> p k i", k=DC) for _ in range(2)]
        w2_sb = [over(IC * D).rearrange("p (k d) -> p k d", k=IC) for _ in range(2)]
        slots_t = [over(DC * C).rearrange("p (k c) -> p k c", k=DC) for _ in range(2)]
        silu_sb = [over(C) for _ in range(2)]
        eh_t = [[sb(f"eh_t{s}_{j}", [P, C]) for j in range(IC)] for s in range(2)]
        w_slot = sb("w_slot", [P, 4, CQ])
        ids = [sb(f"ids{s}", [P, CQ], u32) for s in range(4)]
        near_flat = near[:, :, :, :].rearrange("p s k d -> p (s k d)")
        gathered = [near_flat[:, s * CQ * ROW:(s + 1) * CQ * ROW] for s in range(2)]
        y_flat = more[:, :, :].rearrange("p k d -> p (k d)")
        y_sb = [y_flat[:, s * CQ * D:(s + 1) * CQ * D].rearrange("p (q d) -> p q d", q=CQ) for s in range(2)]
        NQ = NT // 8
        LN_IN = 4
        ln_in = [sign_sb[:, s // 2, (s % 2) * 2 * NQ * D:(s % 2 + 1) * 2 * NQ * D].bitcast(fp32)
                 .rearrange("p (q d) -> p q d", q=NQ) for s in range(LN_IN)]
        ln_out = [near[:, s, :, :] for s in range(2)]
        ln_stats = sb("ln_stats", [P, 2, NQ, 6])
        ln_mv = sb("ln_mv", [P, 2, NQ, 2])
        ln_rstd = sb("ln_rstd", [P, 2, NQ])
        ln_shift = sb("ln_shift", [P, 2, NQ])
        ln_newton_sb = sb("ln_newton_sb", [P, 2, NQ])
        ln_newton = [ln_newton_sb[:, k, :] for k in range(2)]

        bank = [ctx.enter_context(nc.psum_tensor(f"bank{b}", [P, 512], fp32)) for b in range(8)]
        ps_sums = bank[0][:, :].rearrange("p (c t) -> p c t", c=2 * DC)
        ps_z = bank[1]
        ps_tr = bank[2][:, :].rearrange("p (c t) -> p c t", c=IC)
        ps_scores = bank[3][:, 0:E]
        ps_rank = bank[4][:, 0:E]
        ps_full = bank[4][0:1, E:E + ROUNDS]
        ps_h1, ps_h3 = bank[5], bank[6]
        ps_y = bank[7][:, 0:D]
        pe_x = [bank[0], bank[1]]
        pe_h1 = [bank[2], bank[3]]
        pe_h3 = [bank[4], bank[5]]
        pe_y = [bank[6], bank[7]]

        c_pool = sem("c_pool")
        c_dve = sem("c_dve")
        weights_in = sem("weights_in")
        table_in = sem("table_in")
        spare_out = sem("spare_out")
        ln_x_in = [sem(f"ln_x_in{s}") for s in range(LN_IN)]
        ln_link = sem("ln_link")
        ln_scaled = sem("ln_scaled")
        ln_written = sem("ln_written")
        ln_stored = [sem(f"ln_stored{s}") for s in range(2)]
        adj_in = [sem(f"adj_in{s}") for s in range(2)]
        x_in = [sem(f"x_in{s}") for s in range(4)]
        xn_in = [sem(f"xn_in{s}") for s in range(4)]
        sign_done = sem("sign_done")
        near_zeroed = sem("near_zeroed")
        idx_ready = sem("idx_ready")
        full_ready = sem("full_ready")
        full_summed = sem("full_summed")
        flag_ready = sem("flag_ready")
        flag_loaded = sem("flag_loaded")
        nbr_ready = sem("nbr_ready")
        near_in = [[sem(f"near_in{s}_{k}") for k in range(NBR)] for s in range(2)]
        more_in = [sem(f"more_in{k}") for k in range(NBR)]
        more_link = sem("more_link")
        more_idx = sem("more_idx")
        sums_done = sem("sums_done")
        sums_copied = sem("sums_copied")
        proj_done = sem("proj_done")
        z_copied = sem("z_copied")
        z_read = sem("z_read")
        mv_done = sem("mv_done")
        root_link = sem("root_link")
        count_link = sem("count_link")
        x1_link = sem("x1_link")
        xf_done = sem("xf_done")
        xft_done = sem("xft_done")
        xft_copied = sem("xft_copied")
        scores_done = sem("scores_done")
        max_link = sem("max_link")
        max_done = sem("max_done")
        exp_done = sem("exp_done")
        route_link = sem("route_link")
        mask_done = sem("mask_done")
        rank_done = sem("rank_done")
        dest_link = sem("dest_link")
        dest_done = sem("dest_done")
        mask_summed = sem("mask_summed")
        scat = [[sem(f"scat{s}_{k}") for k in range(TOPK)] for s in range(2)]
        scat_drained = sem("scat_drained")
        h_done = sem("h_done")
        tanh_done = sem("tanh_done")
        u_done = sem("u_done")
        g_done = sem("g_done")
        ht_done = sem("ht_done")
        ht_copied = sem("ht_copied")
        y_done = sem("y_done")
        base_done = sem("base_done")
        row_out = [sem(f"row_out{s}") for s in range(4)]
        base_out = [sem(f"base_out{s}") for s in range(2)]
        ids_in = [sem(f"ids_in{s}") for s in range(4)]
        w13_in = [sem(f"w13_in{s}") for s in range(2)]
        w2_in = [sem(f"w2_in{s}") for s in range(2)]
        rows_in = [[sem(f"rows_in{s}_{q}") for q in range(CQ)] for s in range(2)]
        e_xt = [sem(f"e_xt{k}") for k in range(DC)]
        e_xt_copied = [sem(f"e_xt_copied{k}") for k in range(DC)]
        e_w = sem("e_w")
        e_h = sem("e_h")
        e_silu = sem("e_silu")
        e_gated = sem("e_gated")
        e_y = sem("e_y")
        e_y_copied = sem("e_y_copied")
        adds = [sem(f"adds{q}") for q in range(CQ)]
        adds_drained = sem("adds_drained")

        LAG = 4
        ROUTE = 8
        STEPS = NT + LAG
        N_W = 11
        N_POOLC = 12
        CHUNKS = NT // NQ
        x_ln = x.rearrange("(p q) d -> p q d", p=P)
        xn_ln = xn_d.rearrange("(p q) d -> p q d", p=P)
        ELAG = 3
        Tile.UNROLL = 4

        block = ctx.enter_context(nc.Block())

        @block.sync
        def _(sp):
            def ln_load(c):
                if c >= LN_IN:
                    sp.wait_ge(ln_written, c - LN_IN + 1)
                sp.dma_start(ln_in[c % LN_IN], x_ln[:, c * NQ:(c + 1) * NQ, :]).then_inc(ln_x_in[c % LN_IN], 16)

            for c in range(LN_IN):
                ln_load(c)
            for dst, src in ((w_line_sb, w_line_t), (w_nb_sb, w_nb_t), (gate_sb, gate_t),
                             (ws1_sb, ws1), (ws3_sb, ws3), (ws2_sb, ws2)):
                sp.dma_start(dst[:, :, :], src.rearrange("(k p) n -> p k n", p=P)).then_inc(weights_in, 16)
            sp.dma_start(gate_b_sb[:, :], gate_b.rearrange("(a n) -> a n", a=1)).then_inc(weights_in, 16)
            for part, src in enumerate((b_line, b_nb)):
                sp.dma_start(bias_sb[:, part * D:(part + 1) * D], src.rearrange("(a n) -> a n", a=1))\
                  .then_inc(weights_in, 16)
            sp.wait_ge(c_pool, N_POOLC)
            sp.dma_start(table_d.rearrange("(e c) a -> e (c a)", e=E), spare_ids[:, :]).then_inc(table_in, 16)
            sp.dma_start(rows_d[T:T + C, :].rearrange("(p q) n -> p (q n)", p=P), zeros[:, :])\
              .then_inc(spare_out, 16)
            sp.dma_start(out[T:T + C, :].rearrange("(p q) n -> p (q n)", p=P), zeros[:, 0:CQ * D])\
              .then_inc(spare_out, 16)
            for c in range(CHUNKS):
                sp.wait_ge(ln_written, c + 1)
                sp.dma_start(xn_ln[:, c * NQ:(c + 1) * NQ, :], ln_out[c % 2]).then_inc(ln_stored[c % 2], 16)
                if c + LN_IN < CHUNKS:
                    ln_load(c + LN_IN)
            for s in range(2):
                sp.wait_ge(ln_stored[s], 16 * (CHUNKS // 2))

            def step(i, valid):
                if not valid(0):
                    return
                if i.at_least(2):
                    sp.wait_ge(sign_done, i.n - 1)
                sp.dma_start(adj_sb[:, i.slot(2), :], adj[bass.ds(i.n * P, P), :])\
                  .then_inc(adj_in[i.slot(2)], 16)
                if i.at_least(4):
                    sp.wait_ge(xf_done, i.n - 3)
                    sp.wait_ge(sums_done, i.n - 3)
                sp.dma_start(x_sb[:, i.slot(4), :], x[bass.ds(i.n * P, P), :]).then_inc(x_in[i.slot(4)], 16)
                sp.dma_start(xn_sb[:, i.slot(4), :], xn_d[bass.ds(i.n * P, P), :]).then_inc(xn_in[i.slot(4)], 16)

            run_steps(sp, STEPS, NT, LAG, step)

            sp.wait_ge(sign_done, NT)
            for s in range(2):
                for k in range(TOPK):
                    sp.wait_ge(scat[s][k], 16 * (NT // 2))

            def expert(i, valid):
                if not valid(0):
                    return
                if i.at_least(4):
                    sp.wait_ge(adds_drained, i.n - 3)
                sp.dma_start(ids[i.slot(4)][:, :],
                             table_d[bass.ds(i.n * C, C), :].rearrange("(p q) a -> p (q a)", p=P).bitcast(u32))\
                  .then_inc(ids_in[i.slot(4)], 16)
                if i.at_least(2):
                    sp.wait_ge(e_h, IC * (i.n - 1))
                s = i.slot(2)
                for dst, src in ((w1_sb[s], w1), (w3_sb[s], w3)):
                    sp.dma_start(dst, src[bass.ds(i.n, 1), :, :].rearrange("e (k p) n -> p (e k) n", p=P))\
                      .then_inc(w13_in[s], 16)
                if i.at_least(2):
                    sp.wait_ge(e_y, CQ * (i.n - 1))
                sp.dma_start(w2_sb[s], w2[bass.ds(i.n, 1), :, :].rearrange("e (k p) n -> p (e k) n", p=P))\
                  .then_inc(w2_in[s], 16)

            run_steps(sp, E + ELAG, E, ELAG, expert)
            for q in range(CQ):
                sp.wait_ge(adds[q], 16 * E)

        @block.gpsimd
        def _(pool):
            pool.memset(ident[:, :], 0.0).then_inc(c_pool, 1)
            pool.memset(before[:, :], 1.0).then_inc(c_pool, 1)
            pool.memset(ones_bf[:, :], 1.0).then_inc(c_pool, 1)
            pool.memset(ones_row[:, :], 1.0).then_inc(c_pool, 1)
            pool.memset(zeros[:, :], 0.0).then_inc(c_pool, 1)
            pool.wait_ge(c_pool, 5)
            pool.affine_select(out=ident[:, :], in_=ident[:, :], compare_op=ALU.not_equal, fill=1.0,
                               base=0, pattern=[[-1, P]], channel_multiplier=1).then_inc(c_pool, 1)
            pool.affine_select(out=before[:, :], in_=before[:, :], compare_op=ALU.is_gt, fill=0.0,
                               base=0, pattern=[[1, P]], channel_multiplier=-1).then_inc(c_pool, 1)
            pool.iota(token_ids[:, :], pattern=[[P, NT]], base=0, channel_multiplier=1).then_inc(c_pool, 1)
            pool.iota(spare_ids[:, :], pattern=[[1, C]], base=T, channel_multiplier=0).then_inc(c_pool, 1)
            pool.iota(too_many[:, :], pattern=[[2 * NBR, ROUNDS]], base=2 * NBR - T, channel_multiplier=0,
                      allow_small_or_imprecise_dtypes=True).then_inc(c_pool, 1)
            pool.memset(minus_half[:, :], -0.5).then_inc(c_pool, 1)
            pool.iota(slot_code[:, :], pattern=[[-C, E]], base=BIG, channel_multiplier=0,
                      allow_small_or_imprecise_dtypes=True).then_inc(c_pool, 1)

            rounds = pool.alloc_register("pool_more_rounds")
            pool.reg_mov(rounds, 0)
            for s in range(2):
                pool.wait_ge(ln_stored[s], 16 * (CHUNKS // 2))
            pool.wait_ge(table_in, 16)

            def gather(out_ap, idx_ap, signal):
                pool.indirect_dma_start(out=out_ap, out_offset=None, in_=xn_d,
                                        in_offset=bass.IndirectOffsetOnAxis(idx_ap, 0),
                                        bounds_check=T - 1, oob_is_err=False).then_inc(signal, 16)

            def step(i, valid):
                if valid(4):
                    t = i.back(4)
                    if t.at_least(2):
                        for k in range(TOPK):
                            pool.wait_ge(scat[t.slot(2)][k], 16 * t.round(2))
                        pool.nop().then_inc(scat_drained, 1)
                    pool.wait_ge(dest_done, t.n + 1)
                    apart(pool)
                    for k in range(TOPK):
                        pool.indirect_dma_start(
                            out=table_d, out_offset=bass.IndirectOffsetOnAxis(dest[t.slot(4)][:, k:k + 1], 0),
                            in_=token[t.slot(4)][:, :], in_offset=None,
                            bounds_check=E * C - 1, oob_is_err=False).then_inc(scat[t.slot(2)][k], 16)
                if valid(0):
                    pool.wait_ge(idx_ready, i.n + 1)
                    pool.wait_ge(near_zeroed, i.n + 1)
                    apart(pool)
                    for k in range(NBR):
                        gather(near[:, i.slot(2), k, :], idx[i.slot(2)][:, k:k + 1], near_in[i.slot(2)][k])
                    pool.wait_ge(flag_ready, i.n + 1)
                    apart(pool)
                    some = pool.value_load(flags[0:1, 0:1], min_val=0, max_val=P)
                    with pool.If(some > 0):
                        with pool.Fori(0, ROUNDS) as r:
                            again = pool.value_load(flags[0:1, bass.ds(r, 1)], min_val=0, max_val=P)
                            with pool.If(again > 0):
                                pool.reg_add(rounds, rounds, 1)
                                done = pool.snap(rounds, min_val=1, max_val=NT * ROUNDS)
                                pool.wait_ge(more_idx, done)
                                apart(pool)
                                for k in range(NBR):
                                    gather(more[:, k, :], idx_more[:, k:k + 1], more_in[k])
                    pool.nop().then_inc(flag_loaded, 1)

            run_steps(pool, STEPS, NT, LAG, step)

            for s in range(4):
                pool.wait_ge(row_out[s], 16 * (NT // 4))
            for s in range(2):
                pool.wait_ge(base_out[s], 16 * (NT // 2))
            pool.wait_ge(spare_out, 32)
            pool.wait_ge(sums_done, NT)

            def expert(i, valid):
                if valid(3):
                    t = i.back(3)
                    if t.at_least(1):
                        for q in range(CQ):
                            pool.wait_ge(adds[q], 16 * t.n)
                        pool.nop().then_inc(adds_drained, 1)
                    pool.wait_ge(e_y_copied, CQ * (t.n + 1))
                    apart(pool)
                    for q in range(CQ):
                        pool.indirect_dma_start(
                            out=out, out_offset=bass.IndirectOffsetOnAxis(ids[t.slot(4)][:, q:q + 1], 0),
                            in_=y_sb[t.slot(2)][:, q, :], in_offset=None, compute_op=ALU.add)\
                            .then_inc(adds[q], 16)
                if valid(0):
                    s = i.slot(2)
                    pool.wait_ge(ids_in[i.slot(4)], 16 * (i.round(4) + 1))
                    if i.at_least(2):
                        pool.wait_ge(e_xt[1], i.n - 1)
                        pool.wait_ge(e_w, i.n - 1)
                    apart(pool)
                    for q in range(CQ):
                        pool.indirect_dma_start(
                            out=gathered[s][:, q * ROW:(q + 1) * ROW], out_offset=None, in_=rows_d,
                            in_offset=bass.IndirectOffsetOnAxis(ids[i.slot(4)][:, q:q + 1], 0))\
                            .then_inc(rows_in[s][q], 16)

            run_steps(pool, E + ELAG, E, ELAG, expert)

        @block.scalar
        def _(act):
            for c in range(CHUNKS):
                act.wait_ge(ln_scaled, c + 1)
                if c >= 2:
                    act.wait_ge(ln_stored[c % 2], 16 * (c // 2))
                for q in range(NQ):
                    last = act.activation(ln_out[c % 2][:, q, :], ln_in[c % LN_IN][:, q, :], ACT.Identity,
                                          scale=ln_rstd[:, c % 2, q:q + 1], bias=ln_shift[:, c % 2, q:q + 1])
                last.then_inc(ln_written, 1)
            act.wait_ge(c_pool, N_POOLC)
            for s in range(2):
                act.wait_ge(ln_stored[s], 16 * (CHUNKS // 2))

            def zero_near(i):
                if i.at_least(2):
                    act.wait_ge(sums_done, i.n - 1)
                act.activation(near[:, i.slot(2), :, :].rearrange("p k d -> p (k d)"),
                               zeros[:, 0:1].to_broadcast([P, NBR * D]), ACT.Copy).then_inc(near_zeroed, 1)

            def sign(i):
                act.wait_ge(adj_in[i.slot(2)], 16 * (i.round(2) + 1))
                if i.at_least(2):
                    act.wait_ge(nbr_ready, i.n - 1)
                act.activation(sign_sb[:, i.slot(2), 0:T], adj_sb[:, i.slot(2), :], ACT.Sign,
                               bias=minus_half[:, :], scale=1.0,
                               accum_out=sign_sum[:, i.slot(2):i.slot(2) + 1]).then_inc(sign_done, 1)

            def step(i, valid):
                if valid(0):
                    zero_near(i)
                if valid(-1):
                    sign(i.back(-1))
                if valid(3):
                    t = i.back(3)
                    act.wait_ge(max_done, t.n + 1)
                    if t.at_least(1):
                        act.wait_ge(route_link, ROUTE * t.n)
                    act.activation(e_sb[:, :], ps_scores, ACT.Exp, bias=neg_max[:, :], scale=1.0,
                                   accum_out=e_sum[:, :]).then_inc(exp_done, 1)
                if valid(3):
                    t = i.back(3)
                    act.wait_ge(h_done, t.n + 1)
                    if t.at_least(1):
                        act.wait_ge(g_done, t.n)
                    act.activation(tanh_sb[:, :], ps_h1[:, :], ACT.Tanh, scale=0.5).then_inc(tanh_done, 1)
                if valid(1):
                    t = i.back(1)
                    act.wait_ge(sums_done, t.n + 1)
                    if t.at_least(1):
                        act.wait_ge(proj_done, t.n)
                    act.activation(sums_t[:, :, :], ps_sums, ACT.Copy).then_inc(sums_copied, 1)
                if valid(1):
                    t = i.back(1)
                    act.wait_ge(proj_done, t.n + 1)
                    if t.at_least(1):
                        act.wait_ge(z_read, t.n)
                    act.activation(z_sb[:, :], ps_z[:, :], ACT.Copy).then_inc(z_copied, 1)
                if valid(3):
                    t = i.back(3)
                    act.wait_ge(ht_done, t.n + 1)
                    if t.at_least(1):
                        act.wait_ge(y_done, t.n)
                    act.activation(h_t[:, :, :], ps_tr, ACT.Copy).then_inc(ht_copied, 1)
                    act.wait_ge(route_link, ROUTE * (t.n + 1))
                    act.dma_start(rows_d[bass.ds(t.n * P, P), :], row[t.slot(4)][:, :])\
                       .then_inc(row_out[t.slot(4)], 16)
                if valid(4):
                    t = i.back(4)
                    act.wait_ge(base_done, t.n + 1)
                    act.dma_start(out[bass.ds(t.n * P, P), :], base[:, t.slot(2), :])\
                       .then_inc(base_out[t.slot(2)], 16)
                if valid(2):
                    t = i.back(2)
                    act.wait_ge(xft_done, t.n + 1)
                    if t.at_least(1):
                        act.wait_ge(h_done, t.n)
                    act.activation(xf_t[:, :, :], ps_tr[:, 0:DC, :], ACT.Copy).then_inc(xft_copied, 1)

            sign(Tile(0, 0))
            run_steps(act, STEPS, NT, LAG, step)

            def expert(i, valid):
                def silu(t, j):
                    n = IC * t.n + j
                    act.wait_ge(e_h, n + 1)
                    if j >= 2 or t.at_least(1):
                        act.wait_ge(e_gated, n - 1)
                    act.activation(silu_sb[j % 2], pe_h1[j % 2][:, :], ACT.Silu).then_inc(e_silu, 1)

                if valid(1):
                    silu(i.back(1), 0)
                    silu(i.back(1), 1)
                if valid(2):
                    t = i.back(2)
                    act.wait_ge(e_w, t.n + 1)
                    if t.at_least(2):
                        act.wait_ge(adds_drained, t.n - 1)
                    for q in range(CQ):
                        act.wait_ge(e_y, CQ * t.n + q + 1)
                        act.activation(y_sb[t.slot(2)][:, q, :], pe_y[q % 2][:, (q // 2) * D:(q // 2 + 1) * D],
                                       ACT.Copy, scale=w_slot[:, t.slot(4), q:q + 1]).then_inc(e_y_copied, 1)
                if valid(1):
                    silu(i.back(1), 2)
                    silu(i.back(1), 3)
                if valid(0):
                    act.wait_ge(e_xt[0], i.n + 1)
                    if i.at_least(2):
                        act.wait_ge(e_h, IC * (i.n - 1))
                    act.activation(slots_t[i.slot(2)][:, 0, :], pe_x[0][:, :], ACT.Copy)\
                       .then_inc(e_xt_copied[0], 1)

            run_steps(act, E + ELAG, E, ELAG, expert)

        @block.vector
        def _(dve):
            dve.memset(ones8[:, :], 1.0).then_inc(c_dve, 1)
            dve.memset(mask_sum[:, :], 0.0).then_inc(c_dve, 1)
            dve.memset(sign_sb[:, 0, T:T + NBR], 1.0).then_inc(c_dve, 1)
            dve.memset(sign_sb[:, 1, T:T + NBR], 1.0).then_inc(c_dve, 1)
            dve.wait_ge(c_dve, 4)

            ROOT = 3 + 3 * NEWTON

            def root(link, var, y, tmp, steps):
                t, a = tmp
                for k in steps:
                    if k > 0:
                        link.wait()
                    if k == 0:
                        did = dve.tensor_scalar(t, var, EPS, None, ALU.add)
                    elif k == 1:
                        did = dve.tensor_scalar(a.bitcast(i32), t.bitcast(i32), 1, None, ALU.arith_shift_right)
                    elif k == 2:
                        did = dve.tensor_scalar(y.bitcast(i32), a.bitcast(i32), -1.0, float(0x5F3759DF),
                                                ALU.mult, ALU.add)
                    elif k % 3 == 0:
                        did = dve.tensor_tensor(a, y, y, ALU.mult)
                    elif k % 3 == 1:
                        did = dve.scalar_tensor_tensor(out=a, in0=a, scalar=-0.5, in1=t, op0=ALU.mult, op1=ALU.mult)
                    else:
                        did = dve.scalar_tensor_tensor(out=y, in0=a, scalar=1.5, in1=y, op0=ALU.add, op1=ALU.mult)
                    link.did(did)

            ln = Chain(dve, ln_link, 0)
            for c in range(CHUNKS):
                s = c % 2
                dve.wait_ge(ln_x_in[c % LN_IN], 16 * (c // LN_IN + 1))
                if c >= 2:
                    dve.wait_ge(ln_written, c - 1)
                for q in range(NQ):
                    ln.did(dve.bn_stats(ln_stats[:, s, q, :], ln_in[c % LN_IN][:, q, :]))
                ln.wait()
                for q in range(NQ):
                    ln.did(dve.bn_aggr(ln_mv[:, s, q, :], ln_stats[:, s, q, :]))
                ln.wait()
                root(ln, ln_mv[:, s, :, 1], ln_rstd[:, s, :], ln_newton, range(ROOT))
                ln.wait()
                dve.scalar_tensor_tensor(out=ln_shift[:, s, :], in0=ln_mv[:, s, :, 0], scalar=-1.0,
                                         in1=ln_rstd[:, s, :], op0=ALU.mult, op1=ALU.mult).then_inc(ln_scaled, 1)
            dve.wait_ge(c_pool, N_POOLC)
            dve.wait_ge(weights_in, 16 * 9)

            rounds = dve.alloc_register("dve_more_rounds")
            dve.reg_mov(rounds, 0)
            MORE = 12
            COUNT = 4

            def find(i):
                s = i.slot(2)
                link = Chain(dve, count_link, COUNT * i.n)
                dve.wait_ge(sign_done, i.n + 1)
                dve.tensor_scalar(full[:, :], too_many[:, :], sign_sum[:, s:s + 1], None, ALU.is_lt)\
                   .then_inc(full_ready, 1)
                link.did(dve.tensor_scalar(count[:, :], sign_sum[:, s:s + 1], 0.5, 0.5 * T, ALU.mult, ALU.add))
                link.wait()
                link.did(dve.tensor_scalar(cnt1[:, :], count[:, :], 1.0, float(CAP), ALU.max, ALU.min))
                link.did(dve.tensor_scalar(any_nb[:, i.slot(4), :], count[:, :], 1.0, None, ALU.min))
                if i.at_least(2):
                    dve.wait_ge(sums_done, i.n - 1)
                apart(dve)
                dve.max_index(idx[s][:, :], ones8[:, :], sign_sb[:, s, :]).then_inc(idx_ready, 1)
                link.wait()
                link.did(dve.reciprocal(inv_cnt[:, :], cnt1[:, :]))

            def flag_full(i):
                dve.wait_ge(full_summed, i.n + 1)
                if i.at_least(1):
                    dve.wait_ge(flag_loaded, i.n)
                dve.tensor_copy(flags[:, :], ps_full).then_inc(flag_ready, 1)

            def find_more(i):
                s = i.slot(2)
                dve.wait_ge(flag_ready, i.n + 1)
                apart(dve)
                some = dve.value_load(flags[0:1, 0:1], min_val=0, max_val=P)
                with dve.If(some > 0):
                    for k in range(NBR):
                        dve.wait_ge(near_in[s][k], 16 * (i.round(2) + 1))
                    dve.wait_ge(idx_ready, i.n + 1)
                    apart(dve)
                    with dve.Fori(0, ROUNDS) as r:
                        again = dve.value_load(flags[0:1, bass.ds(r, 1)], min_val=0, max_val=P)
                        with dve.If(again > 0):
                            link = Chain(dve, more_link, MORE * dve.snap(rounds, min_val=0, max_val=NT * ROUNDS))
                            link.did(dve.match_replace(sign_sb[:, s, :], ones8[:, :], sign_sb[:, s, :], 0.0))
                            link.did(dve.memset(more[:, :, :], 0.0))
                            link.wait()
                            link.did(dve.memset(sign_sb[:, s, T:T + NBR], 1.0))
                            link.wait()
                            apart(dve)
                            link.did(dve.max_index(idx_more[:, :], ones8[:, :], sign_sb[:, s, :]))
                            link.wait()
                            apart(dve)
                            dve.nop().then_inc(more_idx, 1)
                            dve.reg_add(rounds, rounds, 1)
                            done = dve.snap(rounds, min_val=1, max_val=NT * ROUNDS)
                            for k in range(NBR):
                                dve.wait_ge(more_in[k], 16 * done)
                                link.did(dve.tensor_add(near[:, s, 0, :], near[:, s, 0, :], more[:, k, :]))
                                link.wait()
                            apart(dve)
                            assert link.n == MORE, link.n
                dve.wait_ge(count_link, COUNT * (i.n + 1))
                if i.at_least(1):
                    dve.wait_ge(sums_done, i.n)
                dve.tensor_scalar(mean_diag[:, :], ident[:, :], inv_cnt[:, :], None, ALU.mult)\
                   .then_inc(nbr_ready, 1)

            def row_max(t):
                link = Chain(dve, max_link, t.n)
                dve.wait_ge(scores_done, t.n + 1)
                apart(dve)
                link.did(dve.max(mx8[:, :], ps_scores))
                link.wait()
                dve.tensor_scalar(neg_max[:, :], mx8[:, 0:1], -1.0, None, ALU.mult).then_inc(max_done, 1)

            def graph_layer_and_route(tg, tr):
                if tg:
                    s4 = tg.slot(4)
                    g = Chain(dve, x1_link, 3 * tg.n)
                    dve.wait_ge(z_copied, tg.n + 1)
                    dve.scalar_tensor_tensor(out=lz_sb[:, :], in0=ps_z[:, :], scalar=0.01, in1=z_sb[:, :],
                                             op0=ALU.mult, op1=ALU.max).then_inc(z_read, 1)
                if tr:
                    r = Chain(dve, route_link, ROUTE * tr.n)
                    dve.wait_ge(exp_done, tr.n + 1)
                    r.did(dve.reciprocal(inv_sum[:, :], e_sum[:, :]))
                if tg:
                    dve.wait_ge(z_read, tg.n + 1)
                    dve.wait_ge(x_in[s4], 16 * (tg.round(4) + 1))
                    g.did(dve.tensor_tensor(x1[:, s4, :], x_sb[:, s4, :], lz_sb[:, 0:D], ALU.add))
                if tr:
                    r.wait()
                    r.did(dve.tensor_scalar(probs[:, :], e_sb[:, :], inv_sum[:, :], None, ALU.mult))
                if tg:
                    g.wait()
                    g.did(dve.scalar_tensor_tensor(out=x1[:, s4, :], in0=lz_sb[:, D:2 * D],
                                                   scalar=any_nb[:, s4, :], in1=x1[:, s4, :],
                                                   op0=ALU.mult, op1=ALU.add))
                if tr:
                    r.wait()
                    apart(dve)
                    r.did(dve.max(top8[:, :], probs[:, :]))
                if tg:
                    g.wait()
                    g.did(dve.bn_stats(stats[:, :], x1[:, s4, :]))
                if tr:
                    r.wait()
                    apart(dve)
                    r.did(dve.match_replace(struck[:, :], top8[:, :], probs[:, :], -1.0))
                if tg:
                    g.wait()
                    if tg.at_least(1):
                        dve.wait_ge(xf_done, tg.n)
                    apart(dve)
                    dve.bn_aggr(mv[:, :], stats[:, :]).then_inc(mv_done, 1)
                    assert g.n == 3
                if tr:
                    r.did(dve.tensor_reduce(top_sum[:, :], top8[:, :], AX_X, ALU.add))
                    r.wait()
                    dve.tensor_scalar(mask[:, tr.slot(2), :], struck[:, :], 0.0, None, ALU.is_lt)\
                       .then_inc(mask_done, 1)
                    r.did(dve.tensor_scalar(top_sum_eps[:, :], top_sum[:, :], 1e-8, None, ALU.add))
                    r.wait()
                    r.did(dve.reciprocal(inv_top[:, :], top_sum_eps[:, :]))
                    r.wait()
                    dve.wait_ge(mask_done, tr.n + 1)
                    if tr.at_least(4):
                        dve.wait_ge(row_out[tr.slot(4)], 16 * tr.round(4))
                    r.did(dve.scalar_tensor_tensor(out=row[tr.slot(4)][:, D:ROW], in0=probs[:, :],
                                                   scalar=inv_top[:, :], in1=mask[:, tr.slot(2), :],
                                                   op0=ALU.mult, op1=ALU.mult))
                    assert r.n == ROUTE, r.n

            def second_root(t):
                link = Chain(dve, root_link, ROOT * t.n)

                def one():
                    if link.n == 0:
                        dve.wait_ge(mv_done, t.n + 1)
                    if link.n < ROOT:
                        root(link, mv[:, 1:2], rstd[:, :], (root_sb[:, 0:1], root_sb[:, 1:2]), [link.n])
                return one

            def normalize(t):
                s4 = t.slot(4)
                dve.wait_ge(root_link, ROOT * (t.n + 1))
                if t.at_least(4):
                    dve.wait_ge(row_out[s4], 16 * t.round(4))
                dve.tensor_scalar(row[s4][:, 0:D], x1[:, s4, :], mv[:, 0:1], rstd[:, :],
                                  ALU.subtract, ALU.mult).then_inc(xf_done, 1)

            def gate_hidden(t, between):
                dve.wait_ge(tanh_done, t.n + 1)
                dve.scalar_tensor_tensor(out=u_sb[:, :], in0=tanh_sb[:, :], scalar=1.0,
                                         in1=ps_h1[:, :], op0=ALU.add, op1=ALU.mult).then_inc(u_done, 1)
                between()
                dve.wait_ge(u_done, t.n + 1)
                if t.at_least(1):
                    dve.wait_ge(ht_done, t.n)
                dve.scalar_tensor_tensor(out=g_sb[:, :], in0=u_sb[:, :], scalar=0.5,
                                         in1=ps_h3[:, :], op0=ALU.mult, op1=ALU.mult).then_inc(g_done, 1)

            def destinations(t, between):
                s4 = t.slot(4)
                link = Chain(dve, dest_link, 5 * t.n)
                between()
                if t.at_least(4):
                    dve.wait_ge(scat_drained, t.n - 3)
                link.did(dve.tensor_copy(token[s4][:, :], token_ids[:, bass.ds(t.n, 1)]))
                dve.wait_ge(rank_done, t.n + 1)
                link.did(dve.scalar_tensor_tensor(out=sel[:, :], in0=ps_rank, scalar=float(C),
                                                  in1=mask[:, t.slot(2), :], op0=ALU.is_lt, op1=ALU.mult))
                between()
                link.did(dve.scalar_tensor_tensor(out=code[:, :], in0=ps_rank, scalar=-1.0,
                                                  in1=slot_code[:, :], op0=ALU.mult, op1=ALU.add))
                dve.tensor_tensor(mask_sum[:, :], mask_sum[:, :], mask[:, t.slot(2), :], ALU.add)\
                   .then_inc(mask_summed, 1)
                between()
                link.wait()
                link.did(dve.tensor_tensor(code_sel[:, :], code[:, :], sel[:, :], ALU.mult))
                between()
                link.wait()
                apart(dve)
                link.did(dve.max(code8[:, :], code_sel[:, :]))
                between()
                link.wait()
                dve.tensor_scalar(dest[s4][:, :], code8[:, :], -1.0, float(BIG), ALU.mult, ALU.add)\
                   .then_inc(dest_done, 1)
                assert link.n == 5, link.n

            def add_shared(t):
                dve.wait_ge(y_done, t.n + 1)
                if t.at_least(2):
                    dve.wait_ge(base_out[t.slot(2)], 16 * t.round(2))
                dve.tensor_tensor(base[:, t.slot(2), :], ps_y, x1[:, t.slot(4), :], ALU.add).then_inc(base_done, 1)

            def step(i, valid):
                if valid(0):
                    find(i)
                if valid(3):
                    row_max(i.back(3))
                if valid(0):
                    flag_full(i)
                if valid(2) or valid(3):
                    graph_layer_and_route(i.back(2) if valid(2) else None, i.back(3) if valid(3) else None)
                between = second_root(i.back(2)) if valid(2) else lambda: None
                between()
                if valid(3):
                    gate_hidden(i.back(3), between)
                    destinations(i.back(3), between)
                between()
                if valid(4):
                    add_shared(i.back(4))
                between()
                if valid(0):
                    find_more(i)
                if valid(2):
                    for _ in range(ROOT):
                        between()
                    normalize(i.back(2))

            run_steps(dve, STEPS, NT, LAG, step)

            def expert(i, valid):
                def gated(t, j):
                    n = IC * t.n + j
                    dve.wait_ge(e_silu, n + 1)
                    if t.at_least(2):
                        dve.wait_ge(e_y, CQ * (t.n - 1))
                    dve.tensor_tensor(eh_t[t.slot(2)][j][:, :], silu_sb[j % 2], pe_h3[j % 2][:, :], ALU.mult)\
                       .then_inc(e_gated, 1)

                if valid(1):
                    for j in range(IC):
                        gated(i.back(1), j)
                if valid(0):
                    for q in range(CQ):
                        dve.wait_ge(rows_in[i.slot(2)][q], 16 * (i.round(2) + 1))
                    if i.at_least(4):
                        dve.wait_ge(e_y_copied, CQ * (i.n - 3))
                    weights = gathered[i.slot(2)].rearrange("p (q n) -> p q n", q=CQ)
                    dve.tensor_copy(w_slot[:, i.slot(4), :].rearrange("p (q a) -> p q a", a=1),
                                    weights[:, :, bass.ds(i.n + D, 1)]).then_inc(e_w, 1)
                    dve.wait_ge(e_xt[1], i.n + 1)
                    if i.at_least(2):
                        dve.wait_ge(e_h, IC * (i.n - 1))
                    dve.tensor_copy(slots_t[i.slot(2)][:, 1, :], pe_x[1][:, :]).then_inc(e_xt_copied[1], 1)

            run_steps(dve, E + ELAG, E, ELAG, expert)

        @block.tensor
        def _(pe):
            pe.wait_ge(c_pool, N_POOLC)
            pe.wait_ge(weights_in, 16 * 9)
            pe.wait_ge(c_dve, 4)

            def step(i, valid):
                if valid(1):
                    t = i.back(1)
                    s, s4 = t.slot(2), t.slot(4)
                    pe.wait_ge(xn_in[s4], 16 * (t.round(4) + 1))
                    pe.wait_ge(nbr_ready, t.n + 1)
                    if t.at_least(1):
                        pe.wait_ge(sums_copied, t.n)
                    for h in range(DC):
                        pe.transpose(ps_sums[:, h, :], xn_sb[:, s4, h * P:(h + 1) * P], ident[:, :])
                    for h in range(DC):
                        for k in range(NBR):
                            if h == 0:
                                pe.wait_ge(near_in[s][k], 16 * (t.round(2) + 1))
                            last = pe.matmul(ps_sums[:, DC + h, :], lhsT=near[:, s, k, h * P:(h + 1) * P],
                                             rhs=mean_diag[:, :], start=(k == 0), stop=(k == NBR - 1))
                    last.then_inc(sums_done, 1)
                if valid(0):
                    pe.wait_ge(full_ready, i.n + 1)
                    if i.at_least(1):
                        pe.wait_ge(flag_ready, i.n)
                    pe.matmul(ps_full, lhsT=ones_bf[:, 0:1], rhs=full[:, :], start=True, stop=True)\
                      .then_inc(full_summed, 1)
                if valid(1):
                    t = i.back(1)
                    pe.wait_ge(sums_copied, t.n + 1)
                    if t.at_least(1):
                        pe.wait_ge(z_read, t.n)
                    pe.matmul(ps_z[:, :], lhsT=ones_row[:, :], rhs=bias_sb[:, :], start=True, stop=False)
                    for part, w in enumerate((w_line_sb, w_nb_sb)):
                        for h in range(DC):
                            last = pe.matmul(ps_z[:, part * D:(part + 1) * D], lhsT=sums_t[:, part * DC + h, :],
                                             rhs=w[:, h, :], start=False, stop=(part == 1 and h == DC - 1))
                    last.then_inc(proj_done, 1)
                if valid(3):
                    t = i.back(3)
                    pe.wait_ge(mask_done, t.n + 1)
                    if t.at_least(1):
                        pe.wait_ge(mask_summed, t.n)
                        pe.wait_ge(dest_done, t.n)
                    pe.matmul(ps_rank, lhsT=before[:, :], rhs=mask[:, t.slot(2), :], start=True, stop=False)
                    pe.matmul(ps_rank, lhsT=ones_bf[:, :], rhs=mask_sum[:, :], start=False, stop=True)\
                      .then_inc(rank_done, 1)
                    pe.wait_ge(g_done, t.n + 1)
                    pe.wait_ge(xft_copied, t.n + 1)
                    for h in range(IC):
                        last = pe.transpose(ps_tr[:, h, :], g_sb[:, h * P:(h + 1) * P], ident[:, :])
                    last.then_inc(ht_done, 1)
                    pe.wait_ge(ht_copied, t.n + 1)
                    if t.at_least(1):
                        pe.wait_ge(base_done, t.n)
                    for h in range(IC):
                        last = pe.matmul(ps_y, lhsT=h_t[:, h, :], rhs=ws2_sb[:, h, :],
                                         start=(h == 0), stop=(h == IC - 1))
                    last.then_inc(y_done, 1)
                if valid(2):
                    t = i.back(2)
                    pe.wait_ge(xf_done, t.n + 1)
                    if t.at_least(1):
                        pe.wait_ge(ht_copied, t.n)
                    for h in range(DC):
                        last = pe.transpose(ps_tr[:, h, :], row[t.slot(4)][:, h * P:(h + 1) * P], ident[:, :])
                    last.then_inc(xft_done, 1)
                    pe.wait_ge(xft_copied, t.n + 1)
                    if t.at_least(1):
                        pe.wait_ge(exp_done, t.n)
                    for h in range(DC):
                        pe.matmul(ps_scores, lhsT=xf_t[:, h, :], rhs=gate_sb[:, h, :],
                                  start=(h == 0), stop=False)
                    pe.matmul(ps_scores, lhsT=ones_row[:, :], rhs=gate_b_sb[:, :], start=False, stop=True)\
                      .then_inc(scores_done, 1)
                    if t.at_least(1):
                        pe.wait_ge(g_done, t.n)
                    for ps, w in ((ps_h1, ws1_sb), (ps_h3, ws3_sb)):
                        for h in range(DC):
                            last = pe.matmul(ps[:, :], lhsT=xf_t[:, h, :], rhs=w[:, h, :],
                                             start=(h == 0), stop=(h == DC - 1))
                    last.then_inc(h_done, 1)

            run_steps(pe, STEPS, NT, LAG, step)

            pe.wait_ge(base_done, NT)
            pe.wait_ge(dest_done, NT)

            def expert(i, valid):
                def hidden(t, js):
                    s = t.slot(2)
                    for j in js:
                        n = IC * t.n + j
                        if j == 0:
                            pe.wait_ge(w13_in[s], 32 * (t.round(2) + 1))
                            for k in range(DC):
                                pe.wait_ge(e_xt_copied[k], t.n + 1)
                        if j >= 2 or t.at_least(1):
                            pe.wait_ge(e_gated, n - 1)
                        for ps, w in ((pe_h1, w1_sb), (pe_h3, w3_sb)):
                            for k in range(DC):
                                last = pe.matmul(ps[j % 2][:, :], lhsT=w[s][:, k, j * P:(j + 1) * P],
                                                 rhs=slots_t[s][:, k, :], start=(k == 0), stop=(k == DC - 1))
                        last.then_inc(e_h, 1)

                if valid(1):
                    hidden(i.back(1), (0, 1))
                if valid(2):
                    t = i.back(2)
                    s = t.slot(2)
                    pe.wait_ge(w2_in[s], 16 * (t.round(2) + 1))
                    pe.wait_ge(e_gated, IC * (t.n + 1))
                    for q in range(CQ):
                        if q >= 2 or t.at_least(1):
                            pe.wait_ge(e_y_copied, CQ * t.n + q - 1)
                        for k in range(IC):
                            last = pe.matmul(pe_y[q % 2][:, (q // 2) * D:(q // 2 + 1) * D],
                                             lhsT=eh_t[s][k][:, q * P:(q + 1) * P], rhs=w2_sb[s][:, k, :],
                                             start=(k == 0), stop=(k == IC - 1))
                        last.then_inc(e_y, 1)
                if valid(1):
                    hidden(i.back(1), (2, 3))
                if valid(0):
                    s = i.slot(2)
                    for k in range(DC):
                        if i.at_least(1):
                            pe.wait_ge(e_xt_copied[k], i.n)
                        for q in range(CQ):
                            if k == 0:
                                pe.wait_ge(rows_in[s][q], 16 * (i.round(2) + 1))
                            last = pe.transpose(pe_x[k][:, q * P:(q + 1) * P],
                                                gathered[s][:, q * ROW + k * P:q * ROW + (k + 1) * P], ident[:, :])
                        last.then_inc(e_xt[k], 1)

            run_steps(pe, E + ELAG, E, ELAG, expert)


def kernel(x, adj, L0_gnn_W_nb, L0_gnn_b_nb, L0_gnn_W_line, L0_gnn_b_line, L0_ffn_gate_w,
           L0_ffn_adaptive_bias, L0_ffn_w1, L0_ffn_w3, L0_ffn_w2, L0_ffn_ws1, L0_ffn_ws3, L0_ffn_ws2):
    import numpy as np
    import concourse.bacc as bacc
    from concourse import mybir as mb
    from concourse.bass_utils import run_bass_kernel_spmd

    CAPACITY = 512
    ins = {
        "x": x, "adj": adj,
        "w_nb_t": np.asarray(L0_gnn_W_nb).T, "b_nb": L0_gnn_b_nb,
        "w_line_t": np.asarray(L0_gnn_W_line).T, "b_line": L0_gnn_b_line,
        "gate_t": np.asarray(L0_ffn_gate_w).T, "gate_b": L0_ffn_adaptive_bias,
        "w1": L0_ffn_w1, "w3": L0_ffn_w3, "w2": L0_ffn_w2,
        "ws1": L0_ffn_ws1, "ws3": L0_ffn_ws3, "ws2": L0_ffn_ws2,
    }
    nc = bacc.Bacc("TRN2", target_bir_lowering=False, num_devices=1)
    arrays, args = {}, []
    for name, a in ins.items():
        a = np.ascontiguousarray(a)
        arrays[f"in_{name}"] = a
        args.append(nc.dram_tensor(f"in_{name}", a.shape, mb.dt.from_np(a.dtype), kind="ExternalInput").ap())
    tokens, channels = arrays["in_x"].shape
    args.append(nc.dram_tensor("out_0", (tokens + CAPACITY, channels), mb.dt.float32,
                               kind="ExternalOutput").ap())
    graph_moe_kernel(nc, *args)
    r = run_bass_kernel_spmd(nc, [arrays], core_ids=[0])
    return r.results[0]["out_0"][:tokens]
```

```python
import concourse.bass as bass
from concourse import mybir
from contextlib import ExitStack


class Tile:

    UNROLL = 4

    def __init__(self, g, j):
        self.g, self.j = g + j // self.UNROLL, j % self.UNROLL
        self.n = self.UNROLL * self.g + self.j

    def back(self, lag):
        return Tile(self.g, self.j - lag)

    def slot(self, ring):
        return self.j % ring

    def round(self, ring):
        return (self.UNROLL // ring) * self.g + self.j // ring

    def at_least(self, k):
        return self.n >= k if isinstance(self.n, int) else True


def run_steps(eng, steps, tiles, max_lag, step):
    u = Tile.UNROLL
    assert tiles % u == 0 and max_lag <= u and steps == tiles + max_lag
    for j in range(2 * u):
        step(Tile(0, j), lambda lag, j=j: 0 <= j - lag)
    with eng.Fori(2, tiles // u - 1) as g:
        for j in range(u):
            step(Tile(g, j), lambda lag: True)
    for j in range(u + max_lag):
        step(Tile(tiles // u - 1, j), lambda lag, j=j: j - lag < u)


def apart(eng):
    eng.nop(nofuse=True)


class Chain:

    def __init__(self, eng, sem, base):
        self.eng, self.sem, self.base, self.n = eng, sem, base, 0

    def did(self, instruction):
        instruction.then_inc(self.sem, 1)
        self.n += 1

    def wait(self):
        self.eng.wait_ge(self.sem, self.base + self.n)


def graph_moe_kernel(nc, x, adj, w_nb_t, b_nb, w_line_t, b_line, gate_t, gate_b,
                     w1, w3, w2, ws1, ws3, ws2, out):
    fp32, bf16, i32, u32 = mybir.dt.float32, mybir.dt.bfloat16, mybir.dt.int32, mybir.dt.uint32
    f32r = mybir.dt.float32r
    ALU = mybir.AluOpType
    ACT = mybir.ActivationFunctionType
    AX_X = mybir.AxisListType.X

    P = 128
    T, D = x.shape
    E, _, I = w1.shape
    C = out.shape[0] - T
    NT = T // P
    DC = D // P
    IC = I // P
    CQ = C // P
    TOPK = 8
    NBR = 8
    CAP = 64
    ROUNDS = CAP // NBR - 1
    ROW = D + E
    EPS = 1e-5
    NEWTON = 3
    BIG = 131072
    assert BIG > E * C and DC == 2 and IC == 4 and CQ == 4

    xn_d = nc.dram_tensor("xn_d", (T, D), fp32, kind="Internal").ap()
    rows_d = nc.dram_tensor("rows_d", (T + C, ROW), fp32, kind="Internal").ap()
    table_d = nc.dram_tensor("table_d", (E * C, 1), i32, kind="Internal").ap()

    ctx = ExitStack()
    with ctx:
        def sb(name, shape, dt=fp32):
            return ctx.enter_context(nc.sbuf_tensor(name, shape, dt))

        def sem(name):
            return ctx.enter_context(nc.semaphore(name))

        ident = sb("ident", [P, P])
        before = sb("before", [P, P], bf16)
        ones_bf = sb("ones_bf", [P, P], bf16)
        ones8 = sb("ones8", [P, NBR], bf16)
        ones_row = sb("ones_row", [1, P])
        zeros = sb("zeros", [P, CQ * ROW])
        slot_code = sb("slot_code", [P, E])
        token_ids = sb("token_ids", [P, NT], i32)
        spare_ids = sb("spare_ids", [E, C], i32)
        w_line_sb = sb("w_line_sb", [P, DC, D])
        w_nb_sb = sb("w_nb_sb", [P, DC, D])
        gate_sb = sb("gate_sb", [P, DC, E])
        gate_b_sb = sb("gate_b_sb", [1, E])
        bias_sb = sb("bias_sb", [1, 2 * D])
        ws1_sb = sb("ws1_sb", [P, DC, I])
        ws3_sb = sb("ws3_sb", [P, DC, I])
        ws2_sb = sb("ws2_sb", [P, IC, D])

        w_slot = sb("w_slot", [P, 4, CQ])
        ids = [sb(f"ids{s}", [P, CQ], u32) for s in range(4)]

        tokens = ExitStack()

        def tsb(name, shape, dt=fp32):
            return tokens.enter_context(nc.sbuf_tensor(name, shape, dt))

        adj_sb = tsb("adj_sb", [P, 2, T], i32)
        sign_sb = tsb("sign_sb", [P, 2, T + NBR], bf16)
        near = tsb("near", [P, 2, NBR, D])
        more = tsb("more", [P, NBR, D])
        idx = [tsb(f"idx{s}", [P, NBR], u32) for s in range(2)]
        idx_more = tsb("idx_more", [P, NBR], u32)
        minus_half = tsb("minus_half", [P, 1])
        sign_sum = tsb("sign_sum", [P, 2])
        too_many = tsb("too_many", [P, ROUNDS])
        full = tsb("full", [P, ROUNDS], bf16)
        flags = tsb("flags", [1, ROUNDS], i32)
        count = tsb("count", [P, 1])
        x_sb = tsb("x_sb", [P, 4, D])
        xn_sb = tsb("xn_sb", [P, 4, D])
        sums_t = tsb("sums_t", [P, 2 * DC, P])
        cnt1 = tsb("cnt1", [P, 1])
        inv_cnt = tsb("inv_cnt", [P, 1])
        any_nb = tsb("any_nb", [P, 4, 1])
        mean_diag = tsb("mean_diag", [P, P])
        z_sb = tsb("z_sb", [P, 2 * D])
        lz_sb = tsb("lz_sb", [P, 2 * D])
        x1 = tsb("x1", [P, 4, D])
        stats = tsb("stats", [P, 6])
        mv = tsb("mv", [P, 2])
        rstd = tsb("rstd", [P, 1])
        root_sb = tsb("root_sb", [P, 2])
        row = [tsb(f"row{s}", [P, ROW]) for s in range(4)]
        xf_t = tsb("xf_t", [P, DC, P])
        mx8 = tsb("mx8", [P, 8])
        neg_max = tsb("neg_max", [P, 1])
        e_sb = tsb("e_sb", [P, E])
        e_sum = tsb("e_sum", [P, 1])
        inv_sum = tsb("inv_sum", [P, 1])
        probs = tsb("probs", [P, E])
        top8 = tsb("top8", [P, 8])
        struck = tsb("struck", [P, E])
        mask = tsb("mask", [P, 2, E], bf16)
        mask_sum = tsb("mask_sum", [P, E], bf16)
        top_sum = tsb("top_sum", [P, 1])
        top_sum_eps = tsb("top_sum_eps", [P, 1])
        inv_top = tsb("inv_top", [P, 1])
        sel = tsb("sel", [P, E])
        code = tsb("code", [P, E])
        code_sel = tsb("code_sel", [P, E])
        code8 = tsb("code8", [P, TOPK])
        dest = [tsb(f"dest{s}", [P, TOPK], u32) for s in range(4)]
        token = [tsb(f"token{s}", [P, 1], i32) for s in range(4)]
        tanh_sb = tsb("tanh_sb", [P, I])
        u_sb = tsb("u_sb", [P, I])
        g_sb = tsb("g_sb", [P, I])
        h_t = tsb("h_t", [P, IC, P])
        base = tsb("base", [P, 2, D])

        NQ = NT // 8
        LN_IN = 4
        ln_in = [sign_sb[:, s // 2, (s % 2) * 2 * NQ * D:(s % 2 + 1) * 2 * NQ * D].bitcast(fp32)
                 .rearrange("p (q d) -> p q d", q=NQ) for s in range(LN_IN)]
        LN_OUT = 4
        ln_out = [adj_sb[:, 1, s * NQ * D:(s + 1) * NQ * D].bitcast(fp32)
                  .rearrange("p (q d) -> p q d", q=NQ) for s in range(LN_OUT)]
        ln_stats = tsb("ln_stats", [P, 2, NQ, 6])
        ln_mv = tsb("ln_mv", [P, 2, NQ, 2])
        ln_rstd = tsb("ln_rstd", [P, 2, NQ])
        ln_shift = tsb("ln_shift", [P, 2, NQ])
        ln_newton_sb = tsb("ln_newton_sb", [P, 2, NQ])
        ln_newton = [ln_newton_sb[:, k, :] for k in range(2)]

        tokens.close()
        w13_sb = [sb(f"w13_sb{s}", [P, 2, DC, I]) for s in range(2)]
        w2_sb = [sb(f"w2_sb{s}", [P, IC, D]) for s in range(2)]
        w13_high, w13_low = ([sb(f"w13_{part}{s}", [P, 2, DC, I], f32r) for s in range(2)] for part in ("high", "low"))
        w2_high, w2_low = ([sb(f"w2_{part}{s}", [P, IC, D], f32r) for s in range(2)] for part in ("high", "low"))
        gathered = [sb(f"gathered{s}", [P, CQ, ROW]) for s in range(2)]
        y_sb = [sb(f"y_sb{s}", [P, CQ, D]) for s in range(2)]
        slots_high, slots_low = ([sb(f"slots_{part}{s}", [P, DC, C], f32r) for s in range(2)] for part in ("high", "low"))
        eh_high, eh_low = ([sb(f"eh_{part}{s}", [P, IC, C], f32r) for s in range(2)] for part in ("high", "low"))
        eh_sb = [sb(f"eh_sb{s}", [P, C]) for s in range(2)]
        silu_sb = [sb(f"silu{s}", [P, C]) for s in range(2)]

        bank = [ctx.enter_context(nc.psum_tensor(f"bank{b}", [P, 512], fp32)) for b in range(8)]
        ps_sums = bank[0][:, :].rearrange("p (c t) -> p c t", c=2 * DC)
        ps_z = bank[1]
        ps_tr = bank[2][:, :].rearrange("p (c t) -> p c t", c=IC)
        ps_scores = bank[3][:, 0:E]
        ps_rank = bank[4][:, 0:E]
        ps_full = bank[4][0:1, E:E + ROUNDS]
        ps_h1, ps_h3 = bank[5], bank[6]
        ps_y = bank[7][:, 0:D]
        pe_x = [bank[0], bank[1]]
        pe_h1 = [bank[2], bank[3]]
        pe_h3 = [bank[4], bank[5]]
        pe_y = [bank[6], bank[7]]

        c_pool = sem("c_pool")
        c_dve = sem("c_dve")
        weights_in = sem("weights_in")
        table_in = sem("table_in")
        spare_out = sem("spare_out")
        ln_x_in = [sem(f"ln_x_in{s}") for s in range(LN_IN)]
        ln_stats_link = sem("ln_stats_link")
        ln_link = sem("ln_link")
        ln_scaled = sem("ln_scaled")
        ln_written = sem("ln_written")
        ln_stored = [sem(f"ln_stored{s}") for s in range(LN_OUT)]
        adj_in = [sem(f"adj_in{s}") for s in range(2)]
        x_in = [sem(f"x_in{s}") for s in range(4)]
        xn_in = [sem(f"xn_in{s}") for s in range(4)]
        sign_done = sem("sign_done")
        near_zeroed = sem("near_zeroed")
        idx_ready = sem("idx_ready")
        full_ready = sem("full_ready")
        full_summed = sem("full_summed")
        flag_ready = sem("flag_ready")
        flag_loaded = sem("flag_loaded")
        nbr_ready = sem("nbr_ready")
        near_in = [[sem(f"near_in{s}_{k}") for k in range(NBR)] for s in range(2)]
        more_in = [sem(f"more_in{k}") for k in range(NBR)]
        more_link = sem("more_link")
        more_idx = sem("more_idx")
        sums_done = sem("sums_done")
        sums_copied = sem("sums_copied")
        proj_done = sem("proj_done")
        z_copied = sem("z_copied")
        z_read = sem("z_read")
        mv_done = sem("mv_done")
        root_link = sem("root_link")
        count_link = sem("count_link")
        x1_link = sem("x1_link")
        xf_done = sem("xf_done")
        xft_done = sem("xft_done")
        xft_copied = sem("xft_copied")
        scores_done = sem("scores_done")
        max_link = sem("max_link")
        max_done = sem("max_done")
        exp_done = sem("exp_done")
        route_link = sem("route_link")
        mask_done = sem("mask_done")
        rank_done = sem("rank_done")
        dest_link = sem("dest_link")
        dest_done = sem("dest_done")
        mask_summed = sem("mask_summed")
        scat = [[sem(f"scat{s}_{k}") for k in range(TOPK)] for s in range(2)]
        scat_drained = sem("scat_drained")
        h_done = sem("h_done")
        tanh_done = sem("tanh_done")
        u_done = sem("u_done")
        g_done = sem("g_done")
        ht_done = sem("ht_done")
        ht_copied = sem("ht_copied")
        y_done = sem("y_done")
        base_done = sem("base_done")
        row_out = [sem(f"row_out{s}") for s in range(4)]
        base_out = [sem(f"base_out{s}") for s in range(2)]
        ids_in = [sem(f"ids_in{s}") for s in range(4)]
        w13_in = [sem(f"w13_in{s}") for s in range(2)]
        w2_in = [sem(f"w2_in{s}") for s in range(2)]
        rows_in = [[sem(f"rows_in{s}_{q}") for q in range(CQ)] for s in range(2)]
        w13_rounded = sem("w13_rounded")
        w13_split = sem("w13_split")
        w2_rounded = sem("w2_rounded")
        w2_split = sem("w2_split")
        e_xt = [sem(f"e_xt{k}") for k in range(DC)]
        e_x_rounded = [sem(f"e_x_rounded{k}") for k in range(DC)]
        e_x_split = [sem(f"e_x_split{k}") for k in range(DC)]
        e_w = sem("e_w")
        e_h = sem("e_h")
        e_silu = sem("e_silu")
        e_gated = sem("e_gated")
        e_h_rounded = sem("e_h_rounded")
        e_h_split = sem("e_h_split")
        e_y = sem("e_y")
        e_y_copied = sem("e_y_copied")
        adds = [sem(f"adds{q}") for q in range(CQ)]
        adds_drained = sem("adds_drained")

        LAG = 4
        ROUTE = 8
        STEPS = NT + LAG
        N_W = 9
        N_POOLC = 12
        CHUNKS = NT // NQ
        x_ln = x.rearrange("(p q) d -> p q d", p=P)
        xn_ln = xn_d.rearrange("(p q) d -> p q d", p=P)
        ELAG = 3
        Tile.UNROLL = 4

        block = ctx.enter_context(nc.Block())

        @block.sync
        def _(sp):
            def ln_load(c):
                if c >= LN_IN:
                    sp.wait_ge(ln_written, c - LN_IN + 1)
                sp.dma_start(ln_in[c % LN_IN], x_ln[:, c * NQ:(c + 1) * NQ, :]).then_inc(ln_x_in[c % LN_IN], 16)

            for c in range(LN_IN):
                ln_load(c)
            sp.wait_ge(c_pool, N_POOLC)
            sp.dma_start(table_d.rearrange("(e c) a -> e (c a)", e=E), spare_ids[:, :]).then_inc(table_in, 16)

            def adj_load(i):
                if i.at_least(2):
                    sp.wait_ge(sign_done, i.n - 1)
                sp.dma_start(adj_sb[:, i.slot(2), :], adj[bass.ds(i.n * P, P), :])\
                  .then_inc(adj_in[i.slot(2)], 16)

            for c in range(CHUNKS):
                sp.wait_ge(ln_written, c + 1)
                sp.dma_start(xn_ln[:, c * NQ:(c + 1) * NQ, :], ln_out[c % LN_OUT]).then_inc(ln_stored[c % LN_OUT], 16)
                if c + LN_IN < CHUNKS:
                    ln_load(c + LN_IN)
                if c == 3:
                    adj_load(Tile(0, 0))
            for dst, src in ((w_line_sb, w_line_t), (w_nb_sb, w_nb_t), (gate_sb, gate_t),
                             (ws1_sb, ws1), (ws3_sb, ws3), (ws2_sb, ws2)):
                sp.dma_start(dst[:, :, :], src.rearrange("(k p) n -> p k n", p=P)).then_inc(weights_in, 16)
            sp.dma_start(gate_b_sb[:, :], gate_b.rearrange("(a n) -> a n", a=1)).then_inc(weights_in, 16)
            for part, src in enumerate((b_line, b_nb)):
                sp.dma_start(bias_sb[:, part * D:(part + 1) * D], src.rearrange("(a n) -> a n", a=1))\
                  .then_inc(weights_in, 16)
            sp.dma_start(rows_d[T:T + C, :].rearrange("(p q) n -> p (q n)", p=P), zeros[:, :])\
              .then_inc(spare_out, 16)
            sp.dma_start(out[T:T + C, :].rearrange("(p q) n -> p (q n)", p=P), zeros[:, 0:CQ * D])\
              .then_inc(spare_out, 16)
            for s in range(LN_OUT):
                sp.wait_ge(ln_stored[s], 16 * (CHUNKS // LN_OUT))
            adj_load(Tile(0, 1))

            def step(i, valid):
                if not valid(0):
                    return
                if i.at_least(2):
                    adj_load(i)
                if i.at_least(4):
                    sp.wait_ge(xf_done, i.n - 3)
                    sp.wait_ge(sums_done, i.n - 3)
                sp.dma_start(x_sb[:, i.slot(4), :], x[bass.ds(i.n * P, P), :]).then_inc(x_in[i.slot(4)], 16)
                sp.dma_start(xn_sb[:, i.slot(4), :], xn_d[bass.ds(i.n * P, P), :]).then_inc(xn_in[i.slot(4)], 16)

            run_steps(sp, STEPS, NT, LAG, step)

            sp.wait_ge(sign_done, NT)
            for s in range(2):
                for k in range(TOPK):
                    sp.wait_ge(scat[s][k], 16 * (NT // 2))

            def expert(i, valid):
                if not valid(0):
                    return
                if i.at_least(4):
                    sp.wait_ge(adds_drained, i.n - 3)
                sp.dma_start(ids[i.slot(4)][:, :],
                             table_d[bass.ds(i.n * C, C), :].rearrange("(p q) a -> p (q a)", p=P).bitcast(u32))\
                  .then_inc(ids_in[i.slot(4)], 16)
                if i.at_least(2):
                    sp.wait_ge(w13_split, 2 * (i.n - 1))
                s = i.slot(2)
                for part, src in enumerate((w1, w3)):
                    sp.dma_start(w13_sb[s][:, part, :, :], src[bass.ds(i.n, 1), :, :].rearrange("e (k p) n -> p (e k) n", p=P))\
                      .then_inc(w13_in[s], 16)
                if i.at_least(2):
                    sp.wait_ge(w2_split, i.n - 1)
                sp.dma_start(w2_sb[s][:, :, :], w2[bass.ds(i.n, 1), :, :].rearrange("e (k p) n -> p (e k) n", p=P))\
                  .then_inc(w2_in[s], 16)

            run_steps(sp, E + ELAG, E, ELAG, expert)
            for q in range(CQ):
                sp.wait_ge(adds[q], 16 * E)

        @block.gpsimd
        def _(pool):
            pool.memset(ident[:, :], 0.0).then_inc(c_pool, 1)
            pool.memset(before[:, :], 1.0).then_inc(c_pool, 1)
            pool.memset(ones_bf[:, :], 1.0).then_inc(c_pool, 1)
            pool.memset(ones_row[:, :], 1.0).then_inc(c_pool, 1)
            pool.memset(zeros[:, :], 0.0).then_inc(c_pool, 1)
            pool.wait_ge(c_pool, 5)
            pool.affine_select(out=ident[:, :], in_=ident[:, :], compare_op=ALU.not_equal, fill=1.0,
                               base=0, pattern=[[-1, P]], channel_multiplier=1).then_inc(c_pool, 1)
            pool.affine_select(out=before[:, :], in_=before[:, :], compare_op=ALU.is_gt, fill=0.0,
                               base=0, pattern=[[1, P]], channel_multiplier=-1).then_inc(c_pool, 1)
            pool.iota(token_ids[:, :], pattern=[[P, NT]], base=0, channel_multiplier=1).then_inc(c_pool, 1)
            pool.iota(spare_ids[:, :], pattern=[[1, C]], base=T, channel_multiplier=0).then_inc(c_pool, 1)
            pool.iota(too_many[:, :], pattern=[[2 * NBR, ROUNDS]], base=2 * NBR - T, channel_multiplier=0,
                      allow_small_or_imprecise_dtypes=True).then_inc(c_pool, 1)
            pool.memset(minus_half[:, :], -0.5).then_inc(c_pool, 1)
            pool.iota(slot_code[:, :], pattern=[[-C, E]], base=BIG, channel_multiplier=0,
                      allow_small_or_imprecise_dtypes=True).then_inc(c_pool, 1)

            rounds = pool.alloc_register("pool_more_rounds")
            pool.reg_mov(rounds, 0)
            for s in range(LN_OUT):
                pool.wait_ge(ln_stored[s], 16 * (CHUNKS // LN_OUT))
            pool.wait_ge(table_in, 16)

            def gather(out_ap, idx_ap, signal):
                pool.indirect_dma_start(out=out_ap, out_offset=None, in_=xn_d,
                                        in_offset=bass.IndirectOffsetOnAxis(idx_ap, 0),
                                        bounds_check=T - 1, oob_is_err=False).then_inc(signal, 16)

            def gather_more():
                pool.reg_add(rounds, rounds, 1)
                done = pool.snap(rounds, min_val=1, max_val=NT * ROUNDS)
                pool.wait_ge(more_idx, done)
                apart(pool)
                for k in range(NBR):
                    gather(more[:, k, :], idx_more[:, k:k + 1], more_in[k])

            def step(i, valid):
                if valid(4):
                    t = i.back(4)
                    if t.at_least(2):
                        for k in range(TOPK):
                            pool.wait_ge(scat[t.slot(2)][k], 16 * t.round(2))
                        pool.nop().then_inc(scat_drained, 1)
                    pool.wait_ge(dest_done, t.n + 1)
                    apart(pool)
                    for k in range(TOPK):
                        pool.indirect_dma_start(
                            out=table_d, out_offset=bass.IndirectOffsetOnAxis(dest[t.slot(4)][:, k:k + 1], 0),
                            in_=token[t.slot(4)][:, :], in_offset=None,
                            bounds_check=E * C - 1, oob_is_err=False).then_inc(scat[t.slot(2)][k], 16)
                if valid(0):
                    pool.wait_ge(idx_ready, i.n + 1)
                    pool.wait_ge(near_zeroed, i.n + 1)
                    apart(pool)
                    for k in range(NBR):
                        gather(near[:, i.slot(2), k, :], idx[i.slot(2)][:, k:k + 1], near_in[i.slot(2)][k])
                    pool.wait_ge(flag_ready, i.n + 1)
                    apart(pool)
                    some = pool.value_load(flags[0:1, 0:1], min_val=0, max_val=P)
                    with pool.If(some > 0):
                        gather_more()
                        again = pool.value_load(flags[0:1, 1:2], min_val=0, max_val=P)
                        with pool.If(again > 0):
                            with pool.Fori(1, ROUNDS) as r:
                                again = pool.value_load(flags[0:1, bass.ds(r, 1)], min_val=0, max_val=P)
                                with pool.If(again > 0):
                                    gather_more()
                    pool.nop().then_inc(flag_loaded, 1)

            run_steps(pool, STEPS, NT, LAG, step)

            for s in range(4):
                pool.wait_ge(row_out[s], 16 * (NT // 4))
            for s in range(2):
                pool.wait_ge(base_out[s], 16 * (NT // 2))
            pool.wait_ge(spare_out, 32)
            pool.wait_ge(sums_done, NT)

            def expert(i, valid):
                if valid(4):
                    for q in range(CQ):
                        pool.wait_ge(adds[q], 16 * (i.n - 3))
                    pool.nop().then_inc(adds_drained, 1)
                if valid(0):
                    s = i.slot(2)
                    pool.wait_ge(ids_in[i.slot(4)], 16 * (i.round(4) + 1))
                    if i.at_least(2):
                        pool.wait_ge(e_xt[1], i.n - 1)
                        pool.wait_ge(e_w, i.n - 1)
                    apart(pool)
                    for q in range(CQ):
                        pool.indirect_dma_start(
                            out=gathered[s][:, q, :], out_offset=None, in_=rows_d,
                            in_offset=bass.IndirectOffsetOnAxis(ids[i.slot(4)][:, q:q + 1], 0))\
                            .then_inc(rows_in[s][q], 16)
                if valid(3):
                    t = i.back(3)
                    pool.wait_ge(e_y_copied, CQ * (t.n + 1))
                    apart(pool)
                    for q in range(CQ):
                        pool.indirect_dma_start(
                            out=out, out_offset=bass.IndirectOffsetOnAxis(ids[t.slot(4)][:, q:q + 1], 0),
                            in_=y_sb[t.slot(2)][:, q, :], in_offset=None, compute_op=ALU.add)\
                            .then_inc(adds[q], 16)

            run_steps(pool, E + ELAG, E, ELAG, expert)

        @block.scalar
        def _(act):
            for c in range(CHUNKS):
                act.wait_ge(ln_scaled, c + 1)
                if c >= LN_OUT:
                    act.wait_ge(ln_stored[c % LN_OUT], 16 * (c // LN_OUT))
                for q in range(NQ):
                    last = act.activation(ln_out[c % LN_OUT][:, q, :], ln_in[c % LN_IN][:, q, :], ACT.Identity,
                                          scale=ln_rstd[:, c % 2, q:q + 1], bias=ln_shift[:, c % 2, q:q + 1])
                last.then_inc(ln_written, 1)
            act.wait_ge(c_pool, N_POOLC)

            def zero_near(i):
                if i.at_least(2):
                    act.wait_ge(sums_done, i.n - 1)
                act.activation(near[:, i.slot(2), :, :].rearrange("p k d -> p (k d)"),
                               zeros[:, 0:1].to_broadcast([P, NBR * D]), ACT.Copy).then_inc(near_zeroed, 1)

            def sign(i):
                act.wait_ge(adj_in[i.slot(2)], 16 * (i.round(2) + 1))
                if i.at_least(2):
                    act.wait_ge(nbr_ready, i.n - 1)
                act.activation(sign_sb[:, i.slot(2), 0:T], adj_sb[:, i.slot(2), :], ACT.Sign,
                               bias=minus_half[:, :], scale=1.0,
                               accum_out=sign_sum[:, i.slot(2):i.slot(2) + 1]).then_inc(sign_done, 1)

            def step(i, valid):
                if valid(-1):
                    sign(i.back(-1))
                if valid(3):
                    t = i.back(3)
                    act.wait_ge(max_done, t.n + 1)
                    if t.at_least(1):
                        act.wait_ge(route_link, ROUTE * t.n)
                    act.activation(e_sb[:, :], ps_scores, ACT.Exp, bias=neg_max[:, :], scale=1.0,
                                   accum_out=e_sum[:, :]).then_inc(exp_done, 1)
                if valid(3):
                    t = i.back(3)
                    act.wait_ge(h_done, t.n + 1)
                    if t.at_least(1):
                        act.wait_ge(g_done, t.n)
                    act.activation(tanh_sb[:, :], ps_h1[:, :], ACT.Tanh, scale=0.5).then_inc(tanh_done, 1)
                if valid(1):
                    t = i.back(1)
                    act.wait_ge(sums_done, t.n + 1)
                    if t.at_least(1):
                        act.wait_ge(proj_done, t.n)
                    act.activation(sums_t[:, :, :], ps_sums, ACT.Copy).then_inc(sums_copied, 1)
                if valid(1):
                    t = i.back(1)
                    act.wait_ge(proj_done, t.n + 1)
                    if t.at_least(1):
                        act.wait_ge(z_read, t.n)
                    act.activation(z_sb[:, :], ps_z[:, :], ACT.Copy).then_inc(z_copied, 1)
                if valid(3):
                    t = i.back(3)
                    act.wait_ge(ht_done, t.n + 1)
                    if t.at_least(1):
                        act.wait_ge(y_done, t.n)
                    act.activation(h_t[:, :, :], ps_tr, ACT.Copy).then_inc(ht_copied, 1)
                    act.wait_ge(route_link, ROUTE * (t.n + 1))
                    act.dma_start(rows_d[bass.ds(t.n * P, P), :], row[t.slot(4)][:, :])\
                       .then_inc(row_out[t.slot(4)], 16)
                if valid(4):
                    t = i.back(4)
                    act.wait_ge(base_done, t.n + 1)
                    act.dma_start(out[bass.ds(t.n * P, P), :], base[:, t.slot(2), :])\
                       .then_inc(base_out[t.slot(2)], 16)
                if valid(-1):
                    zero_near(i.back(-1))
                if valid(2):
                    t = i.back(2)
                    act.wait_ge(xft_done, t.n + 1)
                    if t.at_least(1):
                        act.wait_ge(h_done, t.n)
                    act.activation(xf_t[:, :, :], ps_tr[:, 0:DC, :], ACT.Copy).then_inc(xft_copied, 1)

            sign(Tile(0, 0))
            zero_near(Tile(0, 0))
            run_steps(act, STEPS, NT, LAG, step)

            def expert(i, valid):
                def silu(t, j):
                    n = IC * t.n + j
                    act.wait_ge(e_h, n + 1)
                    if j >= 2 or t.at_least(1):
                        act.wait_ge(e_gated, n - 1)
                    act.activation(silu_sb[j % 2][:, :], pe_h1[j % 2][:, :], ACT.Silu).then_inc(e_silu, 1)

                def round_hidden(t, j):
                    act.wait_ge(e_gated, IC * t.n + j + 1)
                    act.activation(eh_high[t.slot(2)][:, j, :], eh_sb[j % 2][:, :], ACT.Copy)\
                       .then_inc(e_h_rounded, 1)

                if valid(1):
                    t = i.back(1)
                    act.wait_ge(w2_in[t.slot(2)], 16 * (t.round(2) + 1))
                    if t.at_least(2):
                        act.wait_ge(e_y, CQ * (t.n - 1))
                    act.activation(w2_high[t.slot(2)][:, :, :], w2_sb[t.slot(2)][:, :, :], ACT.Copy)\
                       .then_inc(w2_rounded, 1)
                    silu(t, 0)
                    silu(t, 1)
                    round_hidden(t, 0)
                    round_hidden(t, 1)
                def round_w13(t, part):
                    act.wait_ge(w13_in[t.slot(2)], 32 * (t.round(2) + 1))
                    act.activation(w13_high[t.slot(2)][:, part, :, :], w13_sb[t.slot(2)][:, part, :, :], ACT.Copy)\
                       .then_inc(w13_rounded, 1)

                if valid(0):
                    s = i.slot(2)
                    for k in range(DC):
                        act.wait_ge(e_xt[k], i.n + 1)
                        if i.at_least(2):
                            act.wait_ge(e_h, IC * (i.n - 1))
                        act.activation(slots_high[s][:, k, :], pe_x[k][:, :], ACT.Copy)\
                           .then_inc(e_x_rounded[k], 1)
                if valid(2):
                    t = i.back(2)
                    act.wait_ge(e_w, t.n + 1)
                    if t.at_least(2):
                        act.wait_ge(adds_drained, t.n - 1)
                    for q in range(CQ):
                        if q >= 2 and valid(0):
                            round_w13(i, q - 2)
                        act.wait_ge(e_y, CQ * t.n + q + 1)
                        act.activation(y_sb[t.slot(2)][:, q, :], pe_y[q % 2][:, (q // 2) * D:(q // 2 + 1) * D],
                                       ACT.Copy, scale=w_slot[:, t.slot(4), q:q + 1]).then_inc(e_y_copied, 1)
                if valid(0) and not valid(2):
                    round_w13(i, 0)
                    round_w13(i, 1)
                if valid(1):
                    t = i.back(1)
                    silu(t, 2)
                    silu(t, 3)
                    round_hidden(t, 2)
                    round_hidden(t, 3)

            run_steps(act, E + ELAG, E, ELAG, expert)

        @block.vector
        def _(dve):
            dve.memset(ones8[:, :], 1.0).then_inc(c_dve, 1)
            dve.memset(mask_sum[:, :], 0.0).then_inc(c_dve, 1)
            dve.memset(sign_sb[:, 0, T:T + NBR], 1.0).then_inc(c_dve, 1)
            dve.memset(sign_sb[:, 1, T:T + NBR], 1.0).then_inc(c_dve, 1)
            dve.wait_ge(c_dve, 4)

            ROOT = 3 + 3 * NEWTON

            def root(link, var, y, tmp, steps):
                t, a = tmp
                for k in steps:
                    if k > 0:
                        link.wait()
                    if k == 0:
                        did = dve.tensor_scalar(t, var, EPS, None, ALU.add)
                    elif k == 1:
                        did = dve.tensor_scalar(a.bitcast(i32), t.bitcast(i32), 1, None, ALU.arith_shift_right)
                    elif k == 2:
                        did = dve.tensor_scalar(y.bitcast(i32), a.bitcast(i32), -1.0, float(0x5F3759DF),
                                                ALU.mult, ALU.add)
                    elif k % 3 == 0:
                        did = dve.tensor_tensor(a, y, y, ALU.mult)
                    elif k % 3 == 1:
                        did = dve.scalar_tensor_tensor(out=a, in0=a, scalar=-0.5, in1=t, op0=ALU.mult, op1=ALU.mult)
                    else:
                        did = dve.scalar_tensor_tensor(out=y, in0=a, scalar=1.5, in1=y, op0=ALU.add, op1=ALU.mult)
                    link.did(did)

            stats_link, ln_root_link = Chain(dve, ln_stats_link, 0), Chain(dve, ln_link, 0)

            def ln_statistics(c, between):
                s = c % 2
                dve.wait_ge(ln_x_in[c % LN_IN], 16 * (c // LN_IN + 1))
                for q in range(NQ):
                    stats_link.did(dve.bn_stats(ln_stats[:, s, q, :], ln_in[c % LN_IN][:, q, :]))
                    between()
                stats_link.wait()
                for q in range(NQ):
                    stats_link.did(dve.bn_aggr(ln_mv[:, s, q, :], ln_stats[:, s, q, :]))
                    if q % 2 == 1:
                        between()

            def ln_scales(c):
                s = c % 2
                steps = iter(range(ROOT + 1))

                def one():
                    k = next(steps, None)
                    if k == 0:
                        stats_link.wait()
                        if c >= 2:
                            dve.wait_ge(ln_written, c - 1)
                    if k is not None and k < ROOT:
                        root(ln_root_link, ln_mv[:, s, :, 1], ln_rstd[:, s, :], ln_newton, [k])
                    elif k == ROOT:
                        ln_root_link.wait()
                        dve.scalar_tensor_tensor(out=ln_shift[:, s, :], in0=ln_mv[:, s, :, 0], scalar=-1.0,
                                                 in1=ln_rstd[:, s, :], op0=ALU.mult, op1=ALU.mult)\
                           .then_inc(ln_scaled, 1)
                return one

            ln_statistics(0, lambda: None)
            for c in range(CHUNKS):
                one = ln_scales(c)
                one()
                if c + 1 < CHUNKS:
                    ln_statistics(c + 1, one)
                for _ in range(ROOT):
                    one()
            dve.wait_ge(c_pool, N_POOLC)

            rounds = dve.alloc_register("dve_more_rounds")
            dve.reg_mov(rounds, 0)
            MORE = 12
            COUNT = 4

            def find(i):
                s = i.slot(2)
                link = Chain(dve, count_link, COUNT * i.n)
                dve.wait_ge(sign_done, i.n + 1)
                link.did(dve.tensor_scalar(count[:, :], sign_sum[:, s:s + 1], 0.5, 0.5 * T, ALU.mult, ALU.add))
                dve.tensor_scalar(full[:, :], too_many[:, :], sign_sum[:, s:s + 1], None, ALU.is_lt)\
                   .then_inc(full_ready, 1)
                link.wait()
                link.did(dve.tensor_scalar(cnt1[:, :], count[:, :], 1.0, float(CAP), ALU.max, ALU.min))
                link.did(dve.tensor_scalar(any_nb[:, i.slot(4), :], count[:, :], 1.0, None, ALU.min))
                if i.at_least(2):
                    dve.wait_ge(sums_done, i.n - 1)
                apart(dve)
                dve.max_index(idx[s][:, :], ones8[:, :], sign_sb[:, s, :]).then_inc(idx_ready, 1)
                link.wait()
                link.did(dve.reciprocal(inv_cnt[:, :], cnt1[:, :]))

            def flag_full(i):
                dve.wait_ge(full_summed, i.n + 1)
                if i.at_least(1):
                    dve.wait_ge(flag_loaded, i.n)
                dve.tensor_copy(flags[:, :], ps_full).then_inc(flag_ready, 1)

            def one_more(i):
                s = i.slot(2)
                link = Chain(dve, more_link, MORE * dve.snap(rounds, min_val=0, max_val=NT * ROUNDS))
                link.did(dve.match_replace(sign_sb[:, s, :], ones8[:, :], sign_sb[:, s, :], 0.0))
                link.did(dve.memset(more[:, :, :], 0.0))
                link.wait()
                link.did(dve.memset(sign_sb[:, s, T:T + NBR], 1.0))
                link.wait()
                apart(dve)
                link.did(dve.max_index(idx_more[:, :], ones8[:, :], sign_sb[:, s, :]))
                link.wait()
                apart(dve)
                dve.nop().then_inc(more_idx, 1)
                dve.reg_add(rounds, rounds, 1)
                done = dve.snap(rounds, min_val=1, max_val=NT * ROUNDS)
                for k in range(NBR):
                    dve.wait_ge(near_in[s][k], 16 * (i.round(2) + 1))
                for k in range(NBR):
                    dve.wait_ge(more_in[k], 16 * done)
                    link.did(dve.tensor_add(near[:, s, 0, :], near[:, s, 0, :], more[:, k, :]))
                    link.wait()
                apart(dve)
                assert link.n == MORE, link.n

            def find_more(i):
                s = i.slot(2)
                dve.wait_ge(flag_ready, i.n + 1)
                apart(dve)
                some = dve.value_load(flags[0:1, 0:1], min_val=0, max_val=P)
                with dve.If(some > 0):
                    dve.wait_ge(idx_ready, i.n + 1)
                    apart(dve)
                    one_more(i)
                    again = dve.value_load(flags[0:1, 1:2], min_val=0, max_val=P)
                    with dve.If(again > 0):
                        with dve.Fori(1, ROUNDS) as r:
                            again = dve.value_load(flags[0:1, bass.ds(r, 1)], min_val=0, max_val=P)
                            with dve.If(again > 0):
                                one_more(i)
                dve.wait_ge(count_link, COUNT * (i.n + 1))
                if i.at_least(1):
                    dve.wait_ge(sums_done, i.n)
                dve.tensor_scalar(mean_diag[:, :], ident[:, :], inv_cnt[:, :], None, ALU.mult)\
                   .then_inc(nbr_ready, 1)

            def row_max(t, beside):
                link = Chain(dve, max_link, t.n)
                dve.wait_ge(scores_done, t.n + 1)
                apart(dve)
                link.did(dve.max(mx8[:, :], ps_scores))
                beside()
                link.wait()
                dve.tensor_scalar(neg_max[:, :], mx8[:, 0:1], -1.0, None, ALU.mult).then_inc(max_done, 1)

            def graph_layer_and_route(tg, tr, between):
                if tg:
                    s4 = tg.slot(4)
                    g = Chain(dve, x1_link, 3 * tg.n)
                    dve.wait_ge(z_copied, tg.n + 1)
                    dve.scalar_tensor_tensor(out=lz_sb[:, :], in0=ps_z[:, :], scalar=0.01, in1=z_sb[:, :],
                                             op0=ALU.mult, op1=ALU.max).then_inc(z_read, 1)
                    dve.wait_ge(z_read, tg.n + 1)
                    dve.wait_ge(x_in[s4], 16 * (tg.round(4) + 1))
                    g.did(dve.tensor_tensor(x1[:, s4, :], x_sb[:, s4, :], lz_sb[:, 0:D], ALU.add))
                if tr:
                    r = Chain(dve, route_link, ROUTE * tr.n)
                    dve.wait_ge(exp_done, tr.n + 1)
                    r.did(dve.reciprocal(inv_sum[:, :], e_sum[:, :]))
                if tg:
                    g.wait()
                    g.did(dve.scalar_tensor_tensor(out=x1[:, s4, :], in0=lz_sb[:, D:2 * D],
                                                   scalar=any_nb[:, s4, :], in1=x1[:, s4, :],
                                                   op0=ALU.mult, op1=ALU.add))
                if tr:
                    r.wait()
                    r.did(dve.tensor_scalar(probs[:, :], e_sb[:, :], inv_sum[:, :], None, ALU.mult))
                if tg:
                    g.wait()
                    g.did(dve.bn_stats(stats[:, :], x1[:, s4, :]))
                if tr:
                    r.wait()
                    apart(dve)
                    r.did(dve.max(top8[:, :], probs[:, :]))
                if tg:
                    g.wait()
                    if tg.at_least(1):
                        dve.wait_ge(xf_done, tg.n)
                    apart(dve)
                    dve.bn_aggr(mv[:, :], stats[:, :]).then_inc(mv_done, 1)
                    assert g.n == 3
                if tr:
                    r.wait()
                    apart(dve)
                    r.did(dve.match_replace(struck[:, :], top8[:, :], probs[:, :], -1.0))
                    r.did(dve.tensor_reduce(top_sum[:, :], top8[:, :], AX_X, ALU.add))
                between()
                if tr:
                    r.wait()
                    dve.tensor_scalar(mask[:, tr.slot(2), :], struck[:, :], 0.0, None, ALU.is_lt)\
                       .then_inc(mask_done, 1)
                    r.did(dve.tensor_scalar(top_sum_eps[:, :], top_sum[:, :], 1e-8, None, ALU.add))
                between()
                if tr:
                    r.wait()
                    r.did(dve.reciprocal(inv_top[:, :], top_sum_eps[:, :]))
                between()
                if tr:
                    r.wait()
                    dve.wait_ge(mask_done, tr.n + 1)
                    if tr.at_least(4):
                        dve.wait_ge(row_out[tr.slot(4)], 16 * tr.round(4))
                    r.did(dve.scalar_tensor_tensor(out=row[tr.slot(4)][:, D:ROW], in0=probs[:, :],
                                                   scalar=inv_top[:, :], in1=mask[:, tr.slot(2), :],
                                                   op0=ALU.mult, op1=ALU.mult))
                    assert r.n == ROUTE, r.n
                between()

            def second_root(t):
                link = Chain(dve, root_link, ROOT * t.n)

                def one():
                    if link.n == 0:
                        dve.wait_ge(mv_done, t.n + 1)
                    if link.n < ROOT:
                        root(link, mv[:, 1:2], rstd[:, :], (root_sb[:, 0:1], root_sb[:, 1:2]), [link.n])
                return one

            def normalize(t):
                s4 = t.slot(4)
                dve.wait_ge(root_link, ROOT * (t.n + 1))
                if t.at_least(4):
                    dve.wait_ge(row_out[s4], 16 * t.round(4))
                dve.tensor_scalar(row[s4][:, 0:D], x1[:, s4, :], mv[:, 0:1], rstd[:, :],
                                  ALU.subtract, ALU.mult).then_inc(xf_done, 1)

            def gate_hidden(t, between):
                dve.wait_ge(tanh_done, t.n + 1)
                dve.scalar_tensor_tensor(out=u_sb[:, :], in0=tanh_sb[:, :], scalar=1.0,
                                         in1=ps_h1[:, :], op0=ALU.add, op1=ALU.mult).then_inc(u_done, 1)
                between()
                dve.wait_ge(u_done, t.n + 1)
                if t.at_least(1):
                    dve.wait_ge(ht_done, t.n)
                dve.scalar_tensor_tensor(out=g_sb[:, :], in0=u_sb[:, :], scalar=0.5,
                                         in1=ps_h3[:, :], op0=ALU.mult, op1=ALU.mult).then_inc(g_done, 1)

            def destinations(t, between):
                s4 = t.slot(4)
                link = Chain(dve, dest_link, 5 * t.n)
                between()
                if t.at_least(4):
                    dve.wait_ge(scat_drained, t.n - 3)
                link.did(dve.tensor_copy(token[s4][:, :], token_ids[:, bass.ds(t.n, 1)]))
                dve.wait_ge(rank_done, t.n + 1)
                link.did(dve.scalar_tensor_tensor(out=sel[:, :], in0=ps_rank, scalar=float(C),
                                                  in1=mask[:, t.slot(2), :], op0=ALU.is_lt, op1=ALU.mult))
                between()
                link.did(dve.scalar_tensor_tensor(out=code[:, :], in0=ps_rank, scalar=-1.0,
                                                  in1=slot_code[:, :], op0=ALU.mult, op1=ALU.add))
                dve.tensor_tensor(mask_sum[:, :], mask_sum[:, :], mask[:, t.slot(2), :], ALU.add)\
                   .then_inc(mask_summed, 1)
                between()
                link.wait()
                link.did(dve.tensor_tensor(code_sel[:, :], code[:, :], sel[:, :], ALU.mult))
                between()
                link.wait()
                apart(dve)
                link.did(dve.max(code8[:, :], code_sel[:, :]))
                between()
                link.wait()
                dve.tensor_scalar(dest[s4][:, :], code8[:, :], -1.0, float(BIG), ALU.mult, ALU.add)\
                   .then_inc(dest_done, 1)
                assert link.n == 5, link.n

            def add_shared(t):
                dve.wait_ge(y_done, t.n + 1)
                if t.at_least(2):
                    dve.wait_ge(base_out[t.slot(2)], 16 * t.round(2))
                dve.tensor_tensor(base[:, t.slot(2), :], ps_y, x1[:, t.slot(4), :], ALU.add).then_inc(base_done, 1)

            def step(i, valid):
                if valid(0):
                    find(i)
                if valid(3):
                    row_max(i.back(3), lambda: flag_full(i) if valid(0) else None)
                elif valid(0):
                    flag_full(i)
                between = second_root(i.back(2)) if valid(2) else lambda: None
                if valid(2) or valid(3):
                    graph_layer_and_route(i.back(2) if valid(2) else None, i.back(3) if valid(3) else None,
                                          between)
                if valid(3):
                    gate_hidden(i.back(3), between)
                    destinations(i.back(3), between)
                between()
                if valid(4):
                    add_shared(i.back(4))
                between()
                if valid(0):
                    find_more(i)
                if valid(2):
                    for _ in range(ROOT):
                        between()
                    normalize(i.back(2))

            run_steps(dve, STEPS, NT, LAG, step)

            def expert(i, valid):
                def low_part(low, high, value):
                    return dve.tensor_tensor(low, value, high.bitcast(fp32), ALU.subtract)

                def gated(t, j):
                    dve.wait_ge(e_silu, IC * t.n + j + 1)
                    if j >= 2 or t.at_least(1):
                        dve.wait_ge(e_h_split, IC * t.n + j - 1)
                    dve.tensor_tensor(eh_sb[j % 2][:, :], silu_sb[j % 2][:, :], pe_h3[j % 2][:, :], ALU.mult)\
                       .then_inc(e_gated, 1)

                def split_hidden(t, j):
                    s = t.slot(2)
                    dve.wait_ge(e_h_rounded, IC * t.n + j + 1)
                    low_part(eh_low[s][:, j, :], eh_high[s][:, j, :], eh_sb[j % 2][:, :]).then_inc(e_h_split, 1)

                if valid(1):
                    t = i.back(1)
                    s = t.slot(2)
                    dve.wait_ge(w2_rounded, t.n + 1)
                    low_part(w2_low[s][:, :, :], w2_high[s][:, :, :], w2_sb[s][:, :, :]).then_inc(w2_split, 1)
                    gated(t, 0)
                    gated(t, 1)
                    split_hidden(t, 0)
                    split_hidden(t, 1)
                if valid(0):
                    s = i.slot(2)
                    for q in range(CQ):
                        dve.wait_ge(rows_in[s][q], 16 * (i.round(2) + 1))
                    if i.at_least(4):
                        dve.wait_ge(e_y_copied, CQ * (i.n - 3))
                    dve.tensor_copy(w_slot[:, i.slot(4), :].rearrange("p (q a) -> p q a", a=1),
                                    gathered[s][:, :, bass.ds(i.n + D, 1)]).then_inc(e_w, 1)
                    for k in range(DC):
                        dve.wait_ge(e_x_rounded[k], i.n + 1)
                        low_part(slots_low[s][:, k, :], slots_high[s][:, k, :], pe_x[k][:, :])\
                            .then_inc(e_x_split[k], 1)
                    for part in range(2):
                        dve.wait_ge(w13_rounded, 2 * i.n + part + 1)
                        low_part(w13_low[s][:, part, :, :], w13_high[s][:, part, :, :], w13_sb[s][:, part, :, :])\
                            .then_inc(w13_split, 1)
                if valid(1):
                    t = i.back(1)
                    gated(t, 2)
                    gated(t, 3)
                    split_hidden(t, 2)
                    split_hidden(t, 3)

            run_steps(dve, E + ELAG, E, ELAG, expert)

        @block.tensor
        def _(pe):
            pe.wait_ge(c_pool, N_POOLC)
            pe.wait_ge(weights_in, 16 * N_W)
            pe.wait_ge(c_dve, 4)

            def count_full(i):
                pe.wait_ge(full_ready, i.n + 1)
                if i.at_least(1):
                    pe.wait_ge(flag_ready, i.n)
                pe.matmul(ps_full, lhsT=ones_bf[:, 0:1], rhs=full[:, :], start=True, stop=True)\
                  .then_inc(full_summed, 1)

            count_full(Tile(0, 0))

            def step(i, valid):
                if valid(1):
                    t = i.back(1)
                    s, s4 = t.slot(2), t.slot(4)
                    pe.wait_ge(xn_in[s4], 16 * (t.round(4) + 1))
                    pe.wait_ge(nbr_ready, t.n + 1)
                    if t.at_least(1):
                        pe.wait_ge(sums_copied, t.n)
                    for h in range(DC):
                        pe.transpose(ps_sums[:, h, :], xn_sb[:, s4, h * P:(h + 1) * P], ident[:, :])
                    for h in range(DC):
                        for k in range(NBR):
                            if h == 0:
                                pe.wait_ge(near_in[s][k], 16 * (t.round(2) + 1))
                            last = pe.matmul(ps_sums[:, DC + h, :], lhsT=near[:, s, k, h * P:(h + 1) * P],
                                             rhs=mean_diag[:, :], start=(k == 0), stop=(k == NBR - 1))
                    last.then_inc(sums_done, 1)
                if valid(1):
                    t = i.back(1)
                    pe.wait_ge(sums_copied, t.n + 1)
                    if t.at_least(1):
                        pe.wait_ge(z_read, t.n)
                    pe.matmul(ps_z[:, :], lhsT=ones_row[:, :], rhs=bias_sb[:, :], start=True, stop=False)
                    for part, w in enumerate((w_line_sb, w_nb_sb)):
                        for h in range(DC):
                            last = pe.matmul(ps_z[:, part * D:(part + 1) * D], lhsT=sums_t[:, part * DC + h, :],
                                             rhs=w[:, h, :], start=False, stop=(part == 1 and h == DC - 1))
                    last.then_inc(proj_done, 1)
                if valid(3):
                    t = i.back(3)
                    pe.wait_ge(mask_done, t.n + 1)
                    if t.at_least(1):
                        pe.wait_ge(mask_summed, t.n)
                        pe.wait_ge(dest_done, t.n)
                    pe.matmul(ps_rank, lhsT=before[:, :], rhs=mask[:, t.slot(2), :], start=True, stop=False)
                    pe.matmul(ps_rank, lhsT=ones_bf[:, :], rhs=mask_sum[:, :], start=False, stop=True)\
                      .then_inc(rank_done, 1)
                    pe.wait_ge(g_done, t.n + 1)
                    pe.wait_ge(xft_copied, t.n + 1)
                    for h in range(IC):
                        last = pe.transpose(ps_tr[:, h, :], g_sb[:, h * P:(h + 1) * P], ident[:, :])
                    last.then_inc(ht_done, 1)
                    pe.wait_ge(ht_copied, t.n + 1)
                    if t.at_least(1):
                        pe.wait_ge(base_done, t.n)
                    for h in range(IC):
                        last = pe.matmul(ps_y, lhsT=h_t[:, h, :], rhs=ws2_sb[:, h, :],
                                         start=(h == 0), stop=(h == IC - 1))
                    last.then_inc(y_done, 1)
                if valid(2):
                    t = i.back(2)
                    pe.wait_ge(xf_done, t.n + 1)
                    if t.at_least(1):
                        pe.wait_ge(ht_copied, t.n)
                    for h in range(DC):
                        last = pe.transpose(ps_tr[:, h, :], row[t.slot(4)][:, h * P:(h + 1) * P], ident[:, :])
                    last.then_inc(xft_done, 1)
                    pe.wait_ge(xft_copied, t.n + 1)
                    if t.at_least(1):
                        pe.wait_ge(exp_done, t.n)
                    for h in range(DC):
                        pe.matmul(ps_scores, lhsT=xf_t[:, h, :], rhs=gate_sb[:, h, :],
                                  start=(h == 0), stop=False)
                    pe.matmul(ps_scores, lhsT=ones_row[:, :], rhs=gate_b_sb[:, :], start=False, stop=True)\
                      .then_inc(scores_done, 1)
                if valid(-1):
                    count_full(i.back(-1))
                if valid(2):
                    t = i.back(2)
                    if t.at_least(1):
                        pe.wait_ge(g_done, t.n)
                    for ps, w in ((ps_h1, ws1_sb), (ps_h3, ws3_sb)):
                        for h in range(DC):
                            last = pe.matmul(ps[:, :], lhsT=xf_t[:, h, :], rhs=w[:, h, :],
                                             start=(h == 0), stop=(h == DC - 1))
                    last.then_inc(h_done, 1)

            run_steps(pe, STEPS, NT, LAG, step)

            pe.wait_ge(base_done, NT)
            pe.wait_ge(dest_done, NT)

            def split_product(ps, lhs, rhs, start, stop):
                (lh, ll), (rh, rl) = lhs, rhs
                pe.matmul(ps, lhsT=lh, rhs=rh, start=start, stop=False)
                pe.matmul(ps, lhsT=lh, rhs=rl, start=False, stop=False)
                return pe.matmul(ps, lhsT=ll, rhs=rh, start=False, stop=stop)

            def expert(i, valid):
                def hidden(t, js):
                    s = t.slot(2)
                    for j in js:
                        n = IC * t.n + j
                        if j == 0:
                            pe.wait_ge(w13_split, 2 * (t.n + 1))
                            for k in range(DC):
                                pe.wait_ge(e_x_split[k], t.n + 1)
                        if j >= 2 or t.at_least(1):
                            pe.wait_ge(e_gated, n - 1)
                        mine = slice(j * P, (j + 1) * P)
                        for part, ps in enumerate((pe_h1, pe_h3)):
                            for k in range(DC):
                                last = split_product(ps[j % 2][:, :], (w13_high[s][:, part, k, mine], w13_low[s][:, part, k, mine]),
                                                     (slots_high[s][:, k, :], slots_low[s][:, k, :]),
                                                     start=(k == 0), stop=(k == DC - 1))
                        last.then_inc(e_h, 1)

                if valid(1):
                    hidden(i.back(1), (0, 1))
                if valid(0):
                    s = i.slot(2)
                    for k in range(DC):
                        if i.at_least(1):
                            pe.wait_ge(e_x_split[k], i.n)
                        for q in range(CQ):
                            if k == 0:
                                pe.wait_ge(rows_in[s][q], 16 * (i.round(2) + 1))
                            last = pe.transpose(pe_x[k][:, q * P:(q + 1) * P],
                                                gathered[s][:, q, k * P:(k + 1) * P], ident[:, :])
                        last.then_inc(e_xt[k], 1)
                if valid(2):
                    t = i.back(2)
                    s = t.slot(2)
                    pe.wait_ge(w2_split, t.n + 1)
                    pe.wait_ge(e_h_split, IC * (t.n + 1))
                    for q in range(CQ):
                        mine = slice(q * P, (q + 1) * P)
                        if q >= 2 or t.at_least(1):
                            pe.wait_ge(e_y_copied, CQ * t.n + q - 1)
                        for k in range(IC):
                            last = split_product(pe_y[q % 2][:, (q // 2) * D:(q // 2 + 1) * D],
                                                 (eh_high[s][:, k, mine], eh_low[s][:, k, mine]),
                                                 (w2_high[s][:, k, :], w2_low[s][:, k, :]),
                                                 start=(k == 0), stop=(k == IC - 1))
                        last.then_inc(e_y, 1)
                if valid(1):
                    hidden(i.back(1), (2, 3))

            run_steps(pe, E + ELAG, E, ELAG, expert)


def kernel(x, adj, L0_gnn_W_nb, L0_gnn_b_nb, L0_gnn_W_line, L0_gnn_b_line, L0_ffn_gate_w,
           L0_ffn_adaptive_bias, L0_ffn_w1, L0_ffn_w3, L0_ffn_w2, L0_ffn_ws1, L0_ffn_ws3, L0_ffn_ws2):
    import numpy as np
    import concourse.bacc as bacc
    from concourse import mybir as mb
    from concourse.bass_utils import run_bass_kernel_spmd

    CAPACITY = 512
    ins = {
        "x": x, "adj": adj,
        "w_nb_t": np.asarray(L0_gnn_W_nb).T, "b_nb": L0_gnn_b_nb,
        "w_line_t": np.asarray(L0_gnn_W_line).T, "b_line": L0_gnn_b_line,
        "gate_t": np.asarray(L0_ffn_gate_w).T, "gate_b": L0_ffn_adaptive_bias,
        "w1": L0_ffn_w1, "w3": L0_ffn_w3, "w2": L0_ffn_w2,
        "ws1": L0_ffn_ws1, "ws3": L0_ffn_ws3, "ws2": L0_ffn_ws2,
    }
    nc = bacc.Bacc("TRN2", target_bir_lowering=False, num_devices=1)
    arrays, args = {}, []
    for name, a in ins.items():
        a = np.ascontiguousarray(a)
        arrays[f"in_{name}"] = a
        args.append(nc.dram_tensor(f"in_{name}", a.shape, mb.dt.from_np(a.dtype), kind="ExternalInput").ap())
    tokens, channels = arrays["in_x"].shape
    args.append(nc.dram_tensor("out_0", (tokens + CAPACITY, channels), mb.dt.float32,
                               kind="ExternalOutput").ap())
    graph_moe_kernel(nc, *args)
    r = run_bass_kernel_spmd(nc, [arrays], core_ids=[0])
    return r.results[0]["out_0"][:tokens]
```
